# Optimizing a Trainium2 kernel written in Bass

```python
import numpy as np
import jax
import jax.numpy as jnp

def _softmax(x, axis=-1):
    return jax.nn.softmax(x, axis=axis)

def _gelu(x):
    return jax.nn.gelu(x, approximate=True)

def _silu(x):
    return jax.nn.silu(x)

def _sigmoid(x):
    return jax.nn.sigmoid(x)

def _layernorm(x, axis=-1, eps=1e-05):
    m = jnp.mean(x, axis=axis, keepdims=True)
    v = jnp.var(x, axis=axis, keepdims=True)
    return (x - m) / jnp.sqrt(v + eps)

def _scatter_add(tgt, idx, src, axis=0):
    return tgt.at[idx].add(src)

def _segment_sum(src, seg, n):
    return jax.ops.segment_sum(src, seg, n)
kernel_name = 'mk_xattn_ffn_d2_seqx_r8_c69909'

def setup_inputs(seed: int=0):
    np.random.seed(seed)
    _w = jnp.asarray

    def _rec_inputs():
        import jax
        import jax.numpy as jnp
        _rk = jax.random.key(seed)
        x = -0.0003929 + 0.9999 * jax.random.normal(jax.random.fold_in(_rk, 1), (128, 64, 128), jnp.float32)
        _lenS = 64 - jax.random.randint(jax.random.fold_in(_rk, 7), (128,), 0, max(1, 64 // 4) + 1, jnp.int32)
        _lenS2 = 64 - jax.random.randint(jax.random.fold_in(_rk, 8), (128,), 0, max(1, 64 // 4) + 1, jnp.int32)
        _ctx_1024P = jax.random.normal(jax.random.fold_in(_rk, 11), (128, 16, 128), jnp.float32)
        _ctx_1024c = jax.random.dirichlet(jax.random.fold_in(_rk, 511), 0.3 * jnp.ones((16,), jnp.float32), (128, 64))
        _ctx_1024t = jnp.einsum('bsk,bkd->bsd', _ctx_1024c, _ctx_1024P)
        _ctx_1024t = _ctx_1024t * jax.lax.rsqrt(jnp.mean(jnp.square(_ctx_1024t)) + 1e-12) * 0.953939
        ctx_1024 = 2.81802e-05 + 1.00001 * (_ctx_1024t + 0.3 * jax.random.normal(jax.random.fold_in(_rk, 611), (128, 64, 128), jnp.float32))
        return (x, ctx_1024)
    x, ctx_1024 = _rec_inputs()

    def _L0_xattn_setup():
        import jax, jax.numpy as jnp
        import numpy as np
        B, L, D = (4, 512, 128)
        key = jax.random.key(seed)
        k1, k2 = jax.random.split(key)
        Q = jax.random.normal(k1, (B, L, D), dtype=jnp.float32)
        K = jax.random.normal(k2, (B, L, D), dtype=jnp.float32)
        return {'Q': Q, 'K': K}
    _L0_xattn_all = _L0_xattn_setup()
    _L0_xattn_in = {k: v for k, v in _L0_xattn_all.items() if k in ()}
    del _L0_xattn_all

    def _L0_ffn_setup():
        import jax, jax.numpy as jnp
        import numpy as np
        D = 128
        H = 128
        E = 8
        K = 2
        I = 2 * 128
        ROUTE_SCALE = 1.0
        key = jax.random.key(seed)
        ks = jax.random.split(key, 12)
        s = lambda *sh: 1.0 / np.sqrt(sh[-1])
        return {'x': jax.random.normal(ks[0], (1, 256, D), jnp.float32), 'gate_w': jax.random.normal(ks[1], (E, D), jnp.float32) * s(E, D), 'w1': jax.random.normal(ks[2], (E, H, D), jnp.float32) * s(H, D), 'b1': jax.random.normal(ks[3], (E, H), jnp.float32) * 0.01, 'w2': jax.random.normal(ks[4], (E, D, H), jnp.float32) * s(D, H), 'b2': jax.random.normal(ks[5], (E, D), jnp.float32) * 0.01, 'w3': jax.random.normal(ks[6], (E, H, D), jnp.float32) * s(H, D), 'b3': jax.random.normal(ks[7], (E, H), jnp.float32) * 0.01, 'sw1': jax.random.normal(ks[8], (I, D), jnp.float32) * s(I, D), 'sw2': jax.random.normal(ks[9], (I, D), jnp.float32) * s(I, D), 'sw3': jax.random.normal(ks[10], (D, I), jnp.float32) * s(D, I)}
    _L0_ffn_all = _L0_ffn_setup()
    _L0_ffn_in = {k: v for k, v in _L0_ffn_all.items() if k in ('gate_w', 'w1', 'b1', 'w2', 'b2', 'w3', 'b3', 'sw1', 'sw2', 'sw3')}
    del _L0_ffn_all

    def _L1_xattn_setup():
        import jax, jax.numpy as jnp
        import numpy as np
        import math
        D_MODEL = 128
        NUM_HEADS = 16
        BATCH, SEQ = (4, 512)
        key = jax.random.key(seed)
        ks = jax.random.split(key, 7)
        s = 1.0 / math.sqrt(D_MODEL)
        return {'query': jax.random.normal(ks[0], (BATCH, SEQ, D_MODEL), jnp.float32), 'value': jax.random.normal(ks[1], (BATCH, SEQ, D_MODEL), jnp.float32), 'Wq': jax.random.normal(ks[2], (D_MODEL, D_MODEL), jnp.float32) * s, 'bq': jax.random.normal(ks[3], (D_MODEL,), jnp.float32) * s, 'qk_b': jnp.zeros((D_MODEL,), jnp.float32), 'Wv': jax.random.normal(ks[4], (D_MODEL, D_MODEL), jnp.float32) * s, 'bv': jax.random.normal(ks[5], (D_MODEL,), jnp.float32) * s}
    _L1_xattn_all = _L1_xattn_setup()
    _L1_xattn_in = {k: v for k, v in _L1_xattn_all.items() if k in ('Wq', 'bq', 'qk_b', 'Wv', 'bv')}
    del _L1_xattn_all

    def _L1_ffn_setup():
        import jax, jax.numpy as jnp
        import numpy as np
        QMAX = 127.0

        def _ste_round(v):
            return v + jax.lax.stop_gradient(jnp.round(v) - v)

        def _act_fake_quant(x, clip_factor):
            scale = jax.nn.sigmoid(clip_factor) * jnp.max(jnp.abs(x)) / QMAX
            return jnp.clip(_ste_round(x / scale), -QMAX - 1.0, QMAX) * scale

        def _weight_fake_quant(w):
            scale = jnp.max(jnp.abs(w), axis=1, keepdims=True) / QMAX
            return jnp.clip(_ste_round(w / scale), -QMAX - 1.0, QMAX) * scale
        key = jax.random.key(seed)
        k1, k2, k3, k4 = jax.random.split(key, 4)
        B, S, H, I = (8, 1024, 128, 352)
        return {'x': jax.random.normal(k1, (B, S, H), dtype=jnp.float32), 'clip_x': jnp.full((1,), 4.0, dtype=jnp.float32), 'clip_down': jnp.full((1,), 4.0, dtype=jnp.float32), 'w_gate': jax.random.normal(k2, (I, H), dtype=jnp.float32) * 0.02, 'w_up': jax.random.normal(k3, (I, H), dtype=jnp.float32) * 0.02, 'w_down': jax.random.normal(k4, (H, I), dtype=jnp.float32) * 0.02}
    _L1_ffn_all = _L1_ffn_setup()
    _L1_ffn_in = {k: v for k, v in _L1_ffn_all.items() if k in ('clip_x', 'clip_down', 'w_gate', 'w_up', 'w_down')}
    del _L1_ffn_all
    return {'x': x, 'ctx_1024': ctx_1024, 'L0_ffn_gate_w': _L0_ffn_in['gate_w'], 'L0_ffn_w1': _L0_ffn_in['w1'], 'L0_ffn_b1': _L0_ffn_in['b1'], 'L0_ffn_w2': _L0_ffn_in['w2'], 'L0_ffn_b2': _L0_ffn_in['b2'], 'L0_ffn_w3': _L0_ffn_in['w3'], 'L0_ffn_b3': _L0_ffn_in['b3'], 'L0_ffn_sw1': _L0_ffn_in['sw1'], 'L0_ffn_sw2': _L0_ffn_in['sw2'], 'L0_ffn_sw3': _L0_ffn_in['sw3'], 'L1_xattn_Wq': _L1_xattn_in['Wq'], 'L1_xattn_bq': _L1_xattn_in['bq'], 'L1_xattn_qk_b': _L1_xattn_in['qk_b'], 'L1_xattn_Wv': _L1_xattn_in['Wv'], 'L1_xattn_bv': _L1_xattn_in['bv'], 'L1_ffn_clip_x': _L1_ffn_in['clip_x'], 'L1_ffn_clip_down': _L1_ffn_in['clip_down'], 'L1_ffn_w_gate': _L1_ffn_in['w_gate'], 'L1_ffn_w_up': _L1_ffn_in['w_up'], 'L1_ffn_w_down': _L1_ffn_in['w_down']}

def reference(x, ctx_1024, L0_ffn_gate_w, L0_ffn_w1, L0_ffn_b1, L0_ffn_w2, L0_ffn_b2, L0_ffn_w3, L0_ffn_b3, L0_ffn_sw1, L0_ffn_sw2, L0_ffn_sw3, L1_xattn_Wq, L1_xattn_bq, L1_xattn_qk_b, L1_xattn_Wv, L1_xattn_bv, L1_ffn_clip_x, L1_ffn_clip_down, L1_ffn_w_gate, L1_ffn_w_up, L1_ffn_w_down):
    import jax
    import jax.numpy as jnp

    def _L0_xattn_ref(Q, K):
        import jax, jax.numpy as jnp
        import numpy as np
        B, L, D = (4, 512, 128)
        scores = jnp.einsum('btd,bsd->bts', K, K)
        Lq = Q.shape[1]
        mask = jnp.tril(jnp.ones((Lq, Lq), dtype=scores.dtype))
        scores = scores * mask[None, :, :]
        Q_proj = jnp.einsum('bts,bsd->btd', scores, Q)
        return Q + Q_proj

    def _L0_ffn_ref(x, gate_w, w1, b1, w2, b2, w3, b3, sw1, sw2, sw3):
        import jax, jax.numpy as jnp
        import numpy as np
        D = 128
        H = 128
        E = 8
        K = 2
        I = 2 * 128
        ROUTE_SCALE = 1.0
        B, S, _ = x.shape
        xt = x.reshape(-1, D)
        logits = xt @ gate_w.T
        scores = jax.nn.softmax(logits.astype(jnp.float32), axis=-1)
        top_vals, idx = jax.lax.top_k(scores, K)
        weights = jnp.take_along_axis(scores, idx, axis=1).astype(x.dtype) * ROUTE_SCALE
        xs = xt[:, None, :] * weights[:, :, None]
        y = jnp.zeros_like(xt)
        for e in range(E):
            mask = (idx == e).astype(x.dtype)
            h = jax.nn.silu(jnp.einsum('tkd,hd->tkh', xs, w1[e]) + b1[e])
            x2 = jnp.einsum('tkh,dh->tkd', h, w2[e]) + b2[e]
            x3 = jnp.einsum('tkd,hd->tkh', xs, w3[e]) + b3[e]
            y = y + jnp.sum(x2 * x3 * mask[:, :, None], axis=1)
        z = jax.nn.silu(xt @ sw1.T) * (xt @ sw2.T) @ sw3.T
        return (y + z).reshape(B, S, D)

    def _L1_xattn_ref(query, value, Wq, bq, qk_b, Wv, bv):
        import jax, jax.numpy as jnp
        import numpy as np
        import math
        D_MODEL = 128
        NUM_HEADS = 16
        BATCH, SEQ = (4, 512)
        q = jnp.einsum('bsd,ed->bse', query, Wq) + bq + qk_b
        v = jnp.einsum('bsd,ed->bse', value, Wv) + bv
        inv_scale = math.sqrt(query.shape[-1] / NUM_HEADS)
        scores = jnp.einsum('bqd,bkd->bqk', q, v) / inv_scale
        attn = jax.nn.softmax(scores, axis=-1)
        return jnp.einsum('bqk,bkd->bqd', attn, v)

    def _L1_ffn_ref(x, clip_x, clip_down, w_gate, w_up, w_down):
        import jax, jax.numpy as jnp
        import numpy as np
        QMAX = 127.0

        def _ste_round(v):
            return v + jax.lax.stop_gradient(jnp.round(v) - v)

        def _act_fake_quant(x, clip_factor):
            scale = jax.nn.sigmoid(clip_factor) * jnp.max(jnp.abs(x)) / QMAX
            return jnp.clip(_ste_round(x / scale), -QMAX - 1.0, QMAX) * scale

        def _weight_fake_quant(w):
            scale = jnp.max(jnp.abs(w), axis=1, keepdims=True) / QMAX
            return jnp.clip(_ste_round(w / scale), -QMAX - 1.0, QMAX) * scale
        xq = _act_fake_quant(x, clip_x[0])
        gate = jnp.einsum('bsh,ih->bsi', xq, _weight_fake_quant(w_gate))
        up = jnp.einsum('bsh,ih->bsi', xq, _weight_fake_quant(w_up))
        h = _act_fake_quant(jax.nn.silu(gate) * up, clip_down[0])
        return jnp.einsum('bsi,hi->bsh', h, _weight_fake_quant(w_down))
    x = x + _L0_xattn_ref(_layernorm(x, axis=-1), ctx_1024)
    x = x + _L0_ffn_ref(_layernorm(x, axis=-1), L0_ffn_gate_w, L0_ffn_w1, L0_ffn_b1, L0_ffn_w2, L0_ffn_b2, L0_ffn_w3, L0_ffn_b3, L0_ffn_sw1, L0_ffn_sw2, L0_ffn_sw3)
    x = x + _L1_xattn_ref(_layernorm(x, axis=-1), ctx_1024, L1_xattn_Wq, L1_xattn_bq, L1_xattn_qk_b, L1_xattn_Wv, L1_xattn_bv)
    x = x + _L1_ffn_ref(_layernorm(x, axis=-1), L1_ffn_clip_x, L1_ffn_clip_down, L1_ffn_w_gate, L1_ffn_w_up, L1_ffn_w_down)
    return x

_drawn_inputs = setup_inputs


def setup_inputs(seed=0):
    import zlib

    import numpy as np

    out = dict(_drawn_inputs(seed))
    spreads = {'L1_xattn_qk_b': (0.0, 2.0)}
    factors = {'L0_ffn_gate_w': 8.0,
     'L0_ffn_w1': 8.0,
     'L0_ffn_b1': 64.0,
     'L0_ffn_w2': 8.0,
     'L0_ffn_b2': 64.0,
     'L0_ffn_w3': 8.0,
     'L0_ffn_b3': 64.0,
     'L0_ffn_sw1': 8.0,
     'L0_ffn_sw2': 8.0,
     'L0_ffn_sw3': 8.0,
     'L1_xattn_Wq': 29.13,
     'L1_xattn_bq': 64.0,
     'L1_xattn_Wv': 26.117,
     'L1_xattn_bv': 64.0,
     'L1_ffn_w_gate': 42.494,
     'L1_ffn_w_up': 38.033,
     'L1_ffn_w_down': 38.348}
    for name, (base, spread) in spreads.items():
        noise = np.random.default_rng([zlib.crc32(name.encode()), seed]).standard_normal(out[name].shape)
        drawn = base * np.exp(spread * noise) if base else spread * noise
        out[name] = jnp.asarray(drawn.astype(out[name].dtype))
    for name, factor in factors.items():
        out[name] = (out[name] * factor).astype(out[name].dtype)
    return out
```

```python
from contextlib import ExitStack

import concourse.bass as bass
from concourse import mybir

fp32 = mybir.dt.float32
fp32r = mybir.dt.float32r
bf16 = mybir.dt.bfloat16
i32 = mybir.dt.int32
ALU = mybir.AluOpType
ACT = mybir.ActivationFunctionType
AX = mybir.AxisListType
RMAX = bass.bass_isa.ReduceOp.max

P = 128
TOK = 8192
SEQ = 64
CH = 512
TPC = CH // P
NCH = TOK // CH
NT = TOK // P
E = 8
NB_FFN = 3
I_FFN = 352
EPS = 1e-5
QMAX = 127.0
MAGIC = 12582912.0
W1, W3, W2, SW1, SW2, SW3 = 0, 8, 16, 24, 26, 28
NW = 30
SCORE_SCALE = (P / 16) ** -0.5


def build(nc, x, ctxT, wall, biases, b3rep, b3pick, gateT, wqT, wvT, wgu, wd, clips, ident, causal, down8, out):
    x_v = x.rearrange("(t p) d -> p t d", p=P)
    out_v = out.rearrange("(t p) d -> p t d", p=P)
    weight_dram = nc.dram_tensor("weight_by_tile", (NT * E, P), fp32).ap()
    mask_dram = nc.dram_tensor("mask_by_tile", (NT * E, P), bf16).ap()

    with ExitStack() as ctx:
        def sb(name, shape, dt=fp32):
            return ctx.enter_context(nc.sbuf_tensor(name, shape, dt))

        def sem(name):
            return ctx.enter_context(nc.semaphore(name))

        X = sb("X", [P, TOK])
        arena = sb("arena", [P, 3 * TOK])
        ctx_t = arena[:, 0:TOK]
        n2_t = arena[:, TOK:2 * TOK]
        misc = arena[:, 2 * TOK:3 * TOK]
        ctx_now = misc[:, 0:512]
        sm = misc[:, 512:1024]
        xn = misc[:, 1024:1536]
        n2 = misc[:, 1536:2048]
        n2_now = misc[:, 2048:2560]
        wstage = misc[:, 3072:3072 + NW * P].rearrange("p (b n) -> p b n", n=P)
        g_tr = misc[:, 0:512]
        g_mtr = misc[:, 512:768].bitcast(bf16)
        wb = misc[:, 0:4096].rearrange("p (h t n) -> p h t n", h=2, t=TPC)
        h_sb = misc[:, 4096:5120].rearrange("p (b n) -> p b n", b=2)
        m3 = misc[:, 5120:7168].rearrange("p (b n) -> p b n", b=4)
        prod = misc[:, 7168:8192].rearrange("p (b n) -> p b n", b=2)
        n3 = n2_t[:, 0:512]
        n3_t = n2_t[:, 512:1024]
        q_t = n2_t[:, 1024:1536]
        v_t = n2_t[:, 1536:2048]
        v_tok = n2_t[:, 2048:2560]
        sc = n2_t[:, 2560:2816].rearrange("p (t k) -> p t k", t=TPC)
        pr = n2_t[:, 3072:3584].rearrange("p (t k) -> p t k", t=TPC)
        pr_t = n2_t[:, 3584:4096]

        wh = sb("wh", [P, NW, P], fp32r)
        wl = sb("wl", [P, NW, P], fp32r)
        nh = sb("nh", [P, CH], fp32r)
        nl = sb("nl", [P, CH], fp32r)
        xh = sb("xh", [P, 2, CH], fp32r)
        xl = sb("xl", [P, 2, CH], fp32r)
        hh = sb("hh", [P, 4, CH], fp32r)
        hl = sb("hl", [P, 4, CH], fp32r)
        gh = sb("gh", [P, 2, CH], fp32r)
        gl = sb("gl", [P, 2, CH], fp32r)
        work = sb("work", [P, 5 * CH])
        ga, gg, zz, yy, yf = (work[:, i * CH:(i + 1) * CH] for i in range(5))
        wgu_f = work[:, 0:768].rearrange("p (b n) -> p b n", n=P)
        wd_f = work[:, 768:1152]
        wgu_q = work[:, 1152:1536].bitcast(bf16)
        wd_q = work[:, 1536:1728].bitcast(bf16)
        wd_diag = work[:, 1792:1920]
        b3a = work[0:24, 1920:2048]
        b3b = work[0:24, 2048:2176]
        b3c = work[0:24, 2176:2304]
        g_sc, g_a, g_b, g_c = (work[:, i * CH:(i + 1) * CH] for i in range(4))
        g_mask = work[:, 2048:2304].bitcast(bf16)
        g_m = work[:, 2304:2368]
        g_r = work[:, 2368:2432]
        qn = work[:, 0:512]
        sg = work[:, 512:2048]
        xq = work[:, 2048:2304].bitcast(bf16)
        hq = work[:, 0:768].bitcast(bf16)
        scaled = work[:, 1024:2048].rearrange("p (b n) -> p b n", b=2)

        b3h = sb("b3h", [24, P], bf16)
        mk = sb("mk", [P, 2 * CH], bf16)
        b3s = sb("b3s", [P, E, P], bf16)
        pick = sb("pick", [24, 3 + E])
        bias = sb("bias", [P, 19])
        bqk = sb("bqk", [P, 1])
        gate_w = sb("gate_w", [P, E])
        wq = sb("wq", [P, P])
        wv = sb("wv", [P, P])
        wgq = sb("wgq", [P, 2 * NB_FFN * P], bf16)
        wdq = sb("wdq", [P, NB_FFN * P], bf16)
        wgu_s = sb("wgu_s", [P, 8])
        wgu_i = sb("wgu_i", [P, 8])
        down_scale = sb("down_scale", [P, P])
        id32 = sb("id32", [P, P])
        id16 = sb("id16", [P, P], bf16)
        cm = sb("cm", [P, P])
        d8 = sb("d8", [P, E])
        ones = sb("ones", [P, P])
        eps_t = sb("eps_t", [P, 1])
        magic_t = sb("magic_t", [P, 1])
        clip = sb("clip", [P, 2])
        sig = sb("sig", [P, 2])
        stat = sb("stat", [P, 2, TPC, 6])
        mv = [sb(f"mv{i}", [P, NT, 2]) for i in range(4)]
        sd = sb("sd", [P, 4, NT])
        rs = sb("rs", [P, 4, NT])
        mv_now = sb("mv_now", [P, 2, TPC, 2])
        nb1 = sb("nb1", [P, NT])
        nb4 = sb("nb4", [P, NT])
        mx = sb("mx", [P, TPC])
        rsum = sb("rsum", [P, TPC])
        rinv = sb("rinv", [P, TPC])
        am = sb("am", [P, 2, NCH])
        qs = sb("qs", [P, 2, 8])

        bank = [ctx.enter_context(nc.psum_tensor(f"bank{i}", [P, CH], fp32)) for i in range(8)]
        bank16 = [b[:, :].bitcast(bf16)[:, 0:CH] for b in bank]
        logits = bank[3][:, :].rearrange("p (t e) -> p t e", e=E)

        LOADS = [(0, 1), (1, 1), (2, 2), (4, 4), (8, 8)]
        x_dma = [sem(f"x_dma{i}") for i in range(len(LOADS))]
        c_dma = [sem(f"c_dma{i}") for i in range(len(LOADS))]
        names = """consts weights_dma small_dma landed pool_consts
            amax_done wscale_done wgu_rounded wd_rounded diag_done wprep_pe wprep_done bqk_done b3_step b3_ready
            stat1_done stats1 sqrt1 recip1 xn_done base_done ctx_copied s_done sm_done o_done x1_done stat2_done stats2
            sqrt2 recip2 n2_done t2_done n2_copied n2_stored logits_done wh_done wl_done
            route shifted exp_g expclip routed_w routed_m route_t_w route_t_m trw_copied trm_copied
            weight_stored mask_stored
            wb_dma0 wb_dma1 mk_dma nh_done nl_done xs_done xh_done xl_done p1_done p3_done p2_done
            silu_done hh_done hl_done m3_done prod_done acc_done ab_done ga_done g_done gh_done gl_done z_done
            zz_done yt_done x2_done stat3_done stats3 sqrt3 recip3 pr_zero
            n3_done t3_done n3t_done vt_pe vt_done qt_pe qt_done v_pe v_done sc_pe max_done sub_done exp_done
            sum_done rinv_done pt_pe pt_done o3_pe x3_done stat4_done stats4 sqrt4 recip4 nb4_done
            n4_act am_done qs_step qs_dve qs_all clamp_done magic_done t4_done xq_done gu_done sg_done
            h_done hmax_done hclamp_done hmagic_done hq_done down_done scaled_done added_done out_dma sp_held dve_held aggr1_done aggr2_done aggr3_done aggr4_done nb1_done centred1 centred2 n4_dve""".split()
        S = {n: sem(n) for n in names}

        def has(c, lag=0):
            return not isinstance(c, int) or 0 <= c - lag < NCH

        def skewed(engine, slot, lag):
            for c in range(lag):
                slot(c)
            with engine.Fori(lag, NCH) as c:
                slot(c)
            for c in range(NCH, NCH + lag):
                slot(c)

        def wait(engine, name, value):
            if not isinstance(value, int) or value > 0:
                engine.wait_ge(S[name], value)

        def tile4(ap):
            return ap.rearrange("p (t n) -> p t n", t=TPC)

        block = ctx.enter_context(nc.Block())

        @block.sync
        def _(sp):
            for dst, src in ((id32, ident), (cm, causal), (gate_w, gateT)):
                sp.dma_start(dst[:, :], src).then_inc(S["consts"], 16)
            for i, (c0, n) in enumerate(LOADS):
                sp.dma_start(X[:, c0 * CH:(c0 + n) * CH].rearrange("p (t d) -> p t d", d=P),
                             x_v[:, c0 * TPC:(c0 + n) * TPC, :]).then_inc(x_dma[i], 16)
                sp.dma_start(ctx_t[:, c0 * CH:(c0 + n) * CH], ctxT[:, c0 * CH:(c0 + n) * CH]).then_inc(c_dma[i], 16)
                if i == 0:
                    small = ((work[:, 0:768], wgu), (wd_f, wd), (wq[:, :], wqT), (wv[:, :], wvT), (bias[:, :], biases),
                             (d8[:, :], down8), (b3a, b3rep), (pick[:, :], b3pick), (clip[:, :], clips.partition_broadcast(P)))
                    for dst, src in small:
                        sp.dma_start(dst, src).then_inc(S["small_dma"], 16)
            sp.dma_start(misc[:, 3072:3072 + NW * P], wall).then_inc(S["weights_dma"], 16)
            sp.wait_ge(S["consts"], 48)
            for i, (c0, n) in enumerate(LOADS):
                sp.wait_ge(x_dma[i], 16)
                sp.wait_ge(c_dma[i], 16)
                sp.sem_inc(S["landed"], n)
            for g in range(4):
                cols = slice(g * P, (g + 1) * P)
                sp.wait_ge(S["trw_copied"], 1)
                sp.dma_start(weight_dram[cols, :], g_tr[:, cols]).then_inc(S["weight_stored"], 16)
                sp.wait_ge(S["trm_copied"], 1)
                sp.dma_start(mask_dram[cols, :], g_mtr[:, cols]).then_inc(S["mask_stored"], 16)
            sp.wait_ge(S["weight_stored"], 64)
            sp.wait_ge(S["mask_stored"], 64)

            w_v = weight_dram.rearrange("(c t e) k -> c t (e k)", t=TPC, e=E)
            k_v = mask_dram.rearrange("(c t e) k -> c e t k", t=TPC, e=E)

            def broadcast(c, half):
                src = w_v[bass.ds(c, 1), :, half * 512:half * 512 + 512]
                src = src.rearrange("c t n -> (c t) n").partition_broadcast(P)
                sp.dma_start(wb[:, half, :, :], src).then_inc(S[f"wb_dma{half}"], 16)

            def masks(c):
                for part in range(3):
                    dst = mk[part * E:(part + 1) * E, bass.ds((c % 2) * CH, CH)].rearrange("e (t k) -> e t k", t=TPC)
                    src = k_v[bass.ds(c, 1), :, :, :].rearrange("c e t k -> (c e) t k")
                    sp.dma_start(dst, src).then_inc(S["mk_dma"], 16)

            sp.wait_ge(S["pool_consts"], 1)
            masks(0)
            sp.wait_ge(S["wl_done"], 1)
            sp.wait_ge(S["wh_done"], 1)
            sp.wait_ge(S["logits_done"], NCH)
            broadcast(0, 0)
            broadcast(0, 1)
            sp.wait_ge(S["mk_dma"], 48)
            masks(1)

            def hold(name, value):
                sp.wait_ge(S[name], value)
                sp.sem_inc(S["sp_held"], 1)

            def next_chunk(c):
                hold("xs_done", E * c - 4)
                broadcast(c, 0)
                hold("xs_done", E * c)
                broadcast(c, 1)

            next_chunk(1)
            with sp.Fori(2, NCH) as c:
                hold("mk_dma", 48 * c)
                hold("p3_done", E * (c - 1))
                masks(c)
                next_chunk(c)

            with sp.Fori(0, NCH) as c:
                hold("added_done", c + 1)
                sp.dma_start(out_v[:, bass.ts(c, TPC), :], X[:, bass.ts(c, CH)].rearrange("p (t d) -> p t d", d=P))\
                    .then_inc(S["out_dma"], 16)
            sp.wait_ge(S["out_dma"], 16 * NCH)

        @block.tensor
        def _(pe):
            mm = nc.tensor.matmul
            pe.sem_inc(S["yt_done"], 1)

            pe.wait_ge(S["consts"], 48)
            pe.wait_ge(S["pool_consts"], 1)
            pe.wait_ge(S["wgu_rounded"], 1)
            for b in range(2 * NB_FFN):
                nc.tensor.transpose(bank16[4 + b // 4][:, b % 4 * P:(b % 4 + 1) * P], wgu_q[:, b * P:(b + 1) * P], id16[:, :])
            pe.wait_ge(S["wd_rounded"], 1)
            for b in range(NB_FFN):
                nc.tensor.transpose(bank16[6][:, b * P:(b + 1) * P], wd_q[:, b * P:(b + 1) * P], id16[:, :])
            pe.wait_ge(S["diag_done"], 1)
            mm(bank[7][:, 0:P], ones[:, :], wd_diag, start=True, stop=True).then_inc(S["wprep_pe"], 1)

            def stage_a(c):
                if has(c):
                    wait(pe, "ctx_copied", c + 1)
                    wait(pe, "sm_done", c)
                    for t in range(TPC):
                        tile = ctx_now[:, t * P:(t + 1) * P]
                        last = mm(bank[0][:, t * P:(t + 1) * P], tile, tile, start=True, stop=True)
                    last.then_inc(S["s_done"], 1)
                if has(c, 1):
                    wait(pe, "sm_done", c)
                    wait(pe, "xn_done", c)
                    wait(pe, "x1_done", c - 1)
                    for t in range(TPC):
                        cols = slice(t * P, (t + 1) * P)
                        last = mm(bank[1][:, cols], sm[:, cols], xn[:, cols], start=True, stop=True)
                    last.then_inc(S["o_done"], 1)
                if has(c, 2):
                    wait(pe, "n2_done", c - 1)
                    wait(pe, "n2_stored", c - 2)
                    for t in range(TPC):
                        cols = slice(t * P, (t + 1) * P)
                        last = nc.tensor.transpose(bank[2][:, cols], n2[:, cols], id32[:, :])
                    last.then_inc(S["t2_done"], 1)
                if has(c, 3):
                    wait(pe, "n2_copied", c - 2)
                    for t in range(TPC):
                        last = mm(bank[3][:, bass.ds(((c - 3) * TPC + t) * E, E)], n2_now[:, t * P:(t + 1) * P],
                                  gate_w[:, :], start=True, stop=True)
                    last.then_inc(S["logits_done"], 1)

            skewed(pe, stage_a, 3)

            pe.wait_ge(S["routed_w"], 1)
            for g in range(4):
                last = nc.tensor.transpose(bank[0][:, g * P:(g + 1) * P], g_a[:, g * P:(g + 1) * P], id32[:, :])
            last.then_inc(S["route_t_w"], 1)
            pe.wait_ge(S["routed_m"], 1)
            for g in range(4):
                last = nc.tensor.transpose(bank16[1][:, g * P:(g + 1) * P], g_mask[:, g * P:(g + 1) * P], id16[:, :])
            last.then_inc(S["route_t_m"], 1)

            def mm3(out, w, hi, lo, start=True, stop=True):
                mm(out, wh[:, w, :], hi, start=start, stop=False)
                mm(out, wh[:, w, :], lo, start=False, stop=False)
                return mm(out, wl[:, w, :], hi, start=False, stop=stop)

            def shared_block(c, i):
                mm3(bank[6][:, :], SW1 + i, nh[:, :], nl[:, :])
                mm3(bank[7][:, :], SW2 + i, nh[:, :], nl[:, :]).then_inc(S["ab_done"], 1)

            def stage_b(c, e):
                n = E * c + e
                here = has(c)
                if here and e == 0:
                    wait(pe, "nh_done", c + 1)
                    wait(pe, "nl_done", c + 1)
                    wait(pe, "zz_done", c)
                    wait(pe, "x2_done", c)
                    wait(pe, "mk_dma", 48 * (c + 1))
                    shared_block(c, 0)
                if here:
                    wait(pe, "xh_done", n + 1)
                    wait(pe, "xl_done", n + 1)
                    wait(pe, "hh_done", n - 1)
                    mm3(bank[2 + e % 2][:, :], W1 + e, xh[:, e % 2, :], xl[:, e % 2, :]).then_inc(S["p1_done"], 1)
                    wait(pe, "m3_done", n)
                    mm3(bank[4][:, :], W3 + e, xh[:, e % 2, :], xl[:, e % 2, :], stop=False)
                    mm(bank[4][:, :], b3s[:, e, :], mk[:, bass.ds((c % 2) * CH, CH)], start=False, stop=True)\
                        .then_inc(S["p3_done"], 1)
                k = (e - 2) % E
                if step_exists(c, e, 2):
                    wait(pe, "hh_done", n - 1)
                    wait(pe, "hl_done", n - 1)
                    wait(pe, "prod_done", n - 2)
                    mm3(bank[5][:, :], W2 + k, hh[:, k % 4, :], hl[:, k % 4, :]).then_inc(S["p2_done"], 1)
                if here and e == 1:
                    wait(pe, "ga_done", 2 * c + 1)
                    wait(pe, "g_done", 2 * c + 1)
                    shared_block(c, 1)
                if here and e == 3:
                    wait(pe, "gl_done", 2 * c + 2)
                    wait(pe, "gh_done", 2 * c + 2)
                    wait(pe, "ga_done", 2 * c + 2)
                    mm3(bank[6][:, :], SW3, gh[:, 0, :], gl[:, 0, :], stop=False)
                    mm3(bank[6][:, :], SW3 + 1, gh[:, 1, :], gl[:, 1, :], start=False).then_inc(S["z_done"], 1)
                if e == 5 and has(c, 1):
                    wait(pe, "acc_done", E * c)
                    if here:
                        wait(pe, "g_done", 2 * c + 2)
                    for t in range(TPC):
                        cols = slice(t * P, (t + 1) * P)
                        last = nc.tensor.transpose(bank[7][:, cols], yf[:, cols], id32[:, :])
                    last.then_inc(S["yt_done"], 1)

            pe.wait_ge(S["wh_done"], 1)
            pe.wait_ge(S["wl_done"], 1)
            pe.wait_ge(S["b3_ready"], 1)
            pe.wait_ge(S["trw_copied"], 1)
            steps(pe, stage_b)

            def stage_c(c):
                if has(c):
                    wait(pe, "n3_done", c + 1)
                    wait(pe, "n3t_done", c)
                    for t in range(TPC):
                        cols = slice(t * P, (t + 1) * P)
                        last = nc.tensor.transpose(bank[0][:, cols], n3[:, cols], id32[:, :])
                    last.then_inc(S["t3_done"], 1)
                    wait(pe, "vt_done", c)
                    mm(bank[1][:, :], wv[:, :], ctx_t[:, bass.ts(c, CH)], start=True, stop=True).then_inc(S["vt_pe"], 1)
                    wait(pe, "n3t_done", c + 1)
                    wait(pe, "qt_done", c)
                    mm(bank[2][:, :], wq[:, :], n3_t, start=True, stop=True).then_inc(S["qt_pe"], 1)
                if has(c, 1):
                    wait(pe, "exp_done", 2 * c)
                    wait(pe, "pt_done", c - 1)
                    for t in range(TPC):
                        last = nc.tensor.transpose(bank[4][:, t * P:(t + 1) * P], pr[:, t, :], id32[:, :])
                    last.then_inc(S["pt_pe"], 1)
                if has(c):
                    wait(pe, "qt_done", c + 1)
                    wait(pe, "vt_done", c + 1)
                    wait(pe, "sub_done", c)
                    for t in range(TPC):
                        for half in range(2):
                            cols = slice(t * P + half * SEQ, t * P + half * SEQ + SEQ)
                            last = mm(bank[5][half * SEQ:(half + 1) * SEQ, t * SEQ:(t + 1) * SEQ], q_t[:, cols],
                                      v_t[:, cols], start=True, stop=True)
                    last.then_inc(S["sc_pe"], 1)
                if has(c, 1):
                    wait(pe, "pt_done", c)
                    wait(pe, "v_done", c)
                    wait(pe, "x3_done", c - 1)
                    for t in range(TPC):
                        cols = slice(t * P, (t + 1) * P)
                        last = mm(bank[6][:, cols], pr_t[:, cols], v_tok[:, cols], start=True, stop=True)
                    last.then_inc(S["o3_pe"], 1)
                if has(c):
                    wait(pe, "v_done", c)
                    for t in range(TPC):
                        cols = slice(t * P, (t + 1) * P)
                        last = nc.tensor.transpose(bank[3][:, cols], v_t[:, cols], id32[:, :])
                    last.then_inc(S["v_pe"], 1)

            skewed(pe, stage_c, 2)

            def stage_d2(c):
                wait(pe, "magic_done", c + 1)
                wait(pe, "xq_done", c)
                for t in range(TPC):
                    cols = slice(t * P, (t + 1) * P)
                    last = nc.tensor.transpose(bank[0][:, cols], qn[:, cols], id32[:, :])
                last.then_inc(S["t4_done"], 1)
                wait(pe, "xq_done", c + 1)
                wait(pe, "h_done", 3 * c)
                for b in range(NB_FFN):
                    for k in (b, NB_FFN + b):
                        last = mm(bank[1 + k][:, :], wgq[:, k * P:(k + 1) * P], xq[:, :], start=True, stop=True)
                    last.then_inc(S["gu_done"], 1)

            stage_d2(0)
            with pe.Fori(1, NCH) as c:
                stage_d2(c)

            def stage_d3(c):
                wait(pe, "hq_done", c + 1)
                wait(pe, "scaled_done", c)
                for t in range(TPC):
                    for b in range(NB_FFN):
                        last = mm(bank[7][:, t * P:(t + 1) * P], hq[:, b * CH + t * P:b * CH + (t + 1) * P],
                                  wdq[:, b * P:(b + 1) * P], start=b == 0, stop=b == NB_FFN - 1)
                last.then_inc(S["down_done"], 1)

            stage_d3(0)
            with pe.Fori(1, NCH) as c:
                stage_d3(c)

        @block.scalar
        def _(act):
            A = nc.scalar.activation

            act.wait_ge(S["pool_consts"], 1)

            def stage_a(c):
                if has(c):
                    wait(act, "landed", c + 1)
                    wait(act, "s_done", c)
                    A(ctx_now, ctx_t[:, bass.ts(c, CH)], ACT.Copy).then_inc(S["ctx_copied"], 1)
                if has(c, 2):
                    wait(act, "stats2", c - 1)
                    A(sd[:, 1, bass.ts(c - 2, TPC)], mv[1][:, bass.ts(c - 2, TPC), 1], ACT.Sqrt, bias=eps_t[:, :])\
                        .then_inc(S["sqrt2"], 1)
                if has(c):
                    wait(act, "stats1", c + 1)
                    A(sd[:, 0, bass.ts(c, TPC)], mv[0][:, bass.ts(c, TPC), 1], ACT.Sqrt, bias=eps_t[:, :])\
                        .then_inc(S["sqrt1"], 1)
                if has(c, 3):
                    wait(act, "t2_done", c - 2)
                    wait(act, "logits_done", c - 3)
                    A(n2_now, bank[2][:, :], ACT.Copy).then_inc(S["n2_copied"], 1)
                    A(n2_t[:, bass.ts(c - 3, CH)], bank[2][:, :], ACT.Copy).then_inc(S["n2_stored"], 1)
                if has(c):
                    wait(act, "nb1_done", c + 1)
                    wait(act, "o_done", c)
                    wait(act, "base_done", c)
                    for t in range(TPC):
                        j = c * TPC + t
                        last = A(xn[:, t * P:(t + 1) * P], X[:, bass.ds(j * P, P)], ACT.Identity,
                                 scale=rs[:, 0, bass.ds(j, 1)], bias=nb1[:, bass.ds(j, 1)])
                    last.then_inc(S["xn_done"], 1)

            for c in range(4):
                stage_a(c)
            act.wait_ge(S["wprep_pe"], 1)
            A(wgq[:, 0:512], bank16[4], ACT.Copy)
            A(wgq[:, 512:768], bank16[5][:, 0:256], ACT.Copy)
            A(wdq[:, :], bank16[6][:, 0:384], ACT.Copy)
            A(down_scale[:, :], bank[7][:, 0:P], ACT.Copy).then_inc(S["wprep_done"], 1)
            with act.Fori(4, NCH) as c:
                stage_a(c)
            act.wait_ge(S["weights_dma"], 16)
            A(wh[:, :, :], wstage, ACT.Copy).then_inc(S["wh_done"], 1)
            for c in range(NCH, NCH + 3):
                stage_a(c)

            act.wait_ge(S["shifted"], 1)
            A(g_sc, g_a, ACT.Exp).then_inc(S["exp_g"], 1)
            act.wait_ge(S["small_dma"], 144)
            A(sig[:, :], clip[:, :], ACT.Exp, scale=-1.0).then_inc(S["expclip"], 1)
            act.wait_ge(S["route_t_w"], 1)
            A(g_tr, bank[0][:, :], ACT.Copy).then_inc(S["trw_copied"], 1)
            act.wait_ge(S["route_t_m"], 1)
            A(g_mtr, bank16[1], ACT.Copy).then_inc(S["trm_copied"], 1)

            def stage_b(c, e):
                n = E * c + e
                here = has(c)
                if here and e == 0:
                    wait(act, "ab_done", 2 * c)
                    A(nh[:, :], n2_t[:, bass.ts(c, CH)], ACT.Copy).then_inc(S["nh_done"], 1)
                if here:
                    wait(act, "xs_done", n + 1)
                    wait(act, "p3_done", n - 1)
                    A(xh[:, e % 2, :], bank[e % 2][:, :], ACT.Copy).then_inc(S["xh_done"], 1)
                if here and e in (1, 3):
                    i = e // 2
                    wait(act, "ab_done", 2 * c + i + 1)
                    wait(act, "g_done", 2 * c + i)
                    A(ga, bank[6][:, :], ACT.Silu).then_inc(S["ga_done"], 1)
                k = (e - 1) % E
                if step_exists(c, e, 1):
                    wait(act, "p1_done", n)
                    wait(act, "hl_done", n - 2)
                    A(h_sb[:, k % 2, :], bank[2 + k % 2][:, :], ACT.Silu, bias=bias[:, k:k + 1]).then_inc(S["silu_done"], 1)
                    wait(act, "p2_done", n - 4)
                    A(hh[:, k % 4, :], bank[2 + k % 2][:, :], ACT.Silu, bias=bias[:, k:k + 1]).then_inc(S["hh_done"], 1)
                    wait(act, "p3_done", n)
                    wait(act, "prod_done", n - 4)
                    A(m3[:, k % 4, :], bank[4][:, :], ACT.Copy).then_inc(S["m3_done"], 1)
                if here and e == 4:
                    wait(act, "z_done", c + 1)
                    wait(act, "acc_done", E * c - 7)
                    A(zz, bank[6][:, :], ACT.Copy).then_inc(S["zz_done"], 1)

            steps(act, stage_b)

            act.wait_ge(S["stats3"], NCH)
            A(sd[:, 2, :], mv[2][:, :, 1], ACT.Sqrt, bias=eps_t[:, :]).then_inc(S["sqrt3"], 1)
            act.wait_ge(S["bqk_done"], 1)
            act.wait_ge(S["pr_zero"], 1)

            def stage_c(c):
                if has(c):
                    wait(act, "t3_done", c + 1)
                    wait(act, "qt_pe", c)
                    A(n3_t, bank[0][:, :], ACT.Copy).then_inc(S["n3t_done"], 1)
                    wait(act, "vt_pe", c + 1)
                    wait(act, "v_pe", c)
                    A(v_t, bank[1][:, :], ACT.Identity, bias=bias[:, 18:19]).then_inc(S["vt_done"], 1)
                    wait(act, "qt_pe", c + 1)
                    wait(act, "sc_pe", c)
                    A(q_t, bank[2][:, :], ACT.Identity, bias=bqk[:, :]).then_inc(S["qt_done"], 1)
                if has(c, 1):
                    wait(act, "pt_pe", c)
                    wait(act, "o3_pe", c - 1)
                    A(pr_t, bank[4][:, :], ACT.Copy).then_inc(S["pt_done"], 1)
                if has(c):
                    wait(act, "sub_done", c + 1)
                    wait(act, "pt_pe", c)
                    wait(act, "sum_done", c)
                    for half in range(2):
                        rows = slice(half * SEQ, (half + 1) * SEQ)
                        A(pr[rows, :, half * SEQ:(half + 1) * SEQ], sc[rows, :, :], ACT.Exp, scale=SCORE_SCALE)\
                            .then_inc(S["exp_done"], 1)
                    wait(act, "v_pe", c + 1)
                    wait(act, "o3_pe", c)
                    A(v_tok, bank[3][:, :], ACT.Copy).then_inc(S["v_done"], 1)

            skewed(act, stage_c, 2)

            act.wait_ge(S["stats4"], NCH)
            A(sd[:, 3, :], mv[3][:, :, 1], ACT.Sqrt, bias=eps_t[:, :]).then_inc(S["sqrt4"], 1)
            act.wait_ge(S["nb4_done"], 1)
            with act.Fori(0, NCH) as c:
                for t in range(2):
                    j = c * TPC + t
                    last = A(arena[:, bass.ds(c * 3 * CH + t * P, P)], X[:, bass.ts(j, P)], ACT.Identity,
                             scale=rs[:, 3, bass.ds(j, 1)], bias=nb4[:, bass.ds(j, 1)])
                last.then_inc(S["n4_act"], 1)
            act.wait_ge(S["qs_dve"], 1)

            def stage_d2(c):
                if has(c):
                    wait(act, "clamp_done", c + 1)
                    wait(act, "t4_done", c)
                    A(qn, arena[:, bass.ds(c * 3 * CH, CH)], ACT.Identity, scale=qs[:, 0, 3:4], bias=magic_t[:, :])\
                        .then_inc(S["magic_done"], 1)
                if has(c, 1):
                    for b in range(NB_FFN):
                        wait(act, "gu_done", 3 * (c - 1) + b + 1)
                        wait(act, "h_done", 3 * (c - 2) + b + 1)
                        A(sg[:, b * CH:(b + 1) * CH], bank[1 + b][:, :], ACT.Silu, scale=wgu_i[:, b:b + 1])\
                            .then_inc(S["sg_done"], 1)

            skewed(act, stage_d2, 2)
            act.wait_ge(S["qs_dve"], 2)
            with act.Fori(0, NCH) as c:
                wait(act, "hclamp_done", c + 1)
                hid = arena[:, bass.ds(c * 3 * CH, 3 * CH)]
                A(hid, hid, ACT.Identity, scale=qs[:, 1, 3:4], bias=magic_t[:, :]).then_inc(S["hmagic_done"], 1)

        @block.vector
        def _(dve):
            V = nc.vector

            dve.sem_inc(S["x2_done"], 1)
            dve.wait_ge(S["small_dma"], 144)
            V.tensor_reduce(wgu_s[:, 0:6], wgu_f, AX.X, ALU.max, apply_absolute_value=True)
            V.tensor_reduce(wgu_s[:, 6:7], wd_f, AX.X, ALU.max, apply_absolute_value=True).then_inc(S["amax_done"], 1)
            dve.wait_ge(S["amax_done"], 1)
            V.tensor_scalar(wgu_s[:, 0:7], wgu_s[:, 0:7], 1e-30, 1.0 / QMAX, ALU.max, ALU.mult).then_inc(S["amax_done"], 1)
            dve.wait_ge(S["amax_done"], 2)
            V.reciprocal(wgu_i[:, 0:7], wgu_s[:, 0:7]).then_inc(S["wscale_done"], 1)
            dve.wait_ge(S["wscale_done"], 1)
            for b in range(2 * NB_FFN):
                V.tensor_scalar(wgu_f[:, b, :], wgu_f[:, b, :], wgu_i[:, b:b + 1], MAGIC, ALU.mult, ALU.add)
            V.tensor_scalar(wd_f, wd_f, wgu_i[:, 6:7], MAGIC, ALU.mult, ALU.add).then_inc(S["wscale_done"], 1)
            dve.wait_ge(S["wscale_done"], 2)
            V.tensor_scalar(wgu_q, work[:, 0:768], MAGIC, None, ALU.subtract).then_inc(S["wgu_rounded"], 1)
            V.tensor_scalar(wd_q, wd_f, MAGIC, None, ALU.subtract).then_inc(S["wd_rounded"], 1)
            dve.wait_ge(S["consts"], 48)
            V.tensor_scalar(wd_diag, id32[:, :], wgu_s[:, 6:7], None, ALU.mult).then_inc(S["diag_done"], 1)
            V.tensor_tensor(bqk[:, :], bias[:, 16:17], bias[:, 17:18], ALU.add).then_inc(S["bqk_done"], 1)

            def stats(norm, c):
                for t in range(TPC):
                    last = V.bn_stats(stat[:, norm % 2, t, :], X[:, bass.ds((c * TPC + t) * P, P)])
                last.then_inc(S[f"stat{norm + 1}_done"], 1)
                dve.wait_ge(S[f"stat{norm + 1}_done"], c + 1)
                dve.sem_inc(S["dve_held"], 1)
                for t in range(TPC):
                    last = V.bn_aggr(mv_now[:, norm % 2, t, :], stat[:, norm % 2, t, :])
                last.then_inc(S[f"aggr{norm + 1}_done"], 1)
                dve.wait_ge(S[f"aggr{norm + 1}_done"], c + 1)
                V.tensor_copy(mv[norm][:, bass.ds(c * TPC, TPC), :], mv_now[:, norm % 2, :, :]).then_inc(S[f"stats{norm + 1}"], 1)

            def stage_a(c):
                if has(c, 2):
                    wait(dve, "o_done", c - 1)
                    wait(dve, "base_done", c - 1)
                    cols = bass.ts(c - 2, CH)
                    V.tensor_tensor(X[:, cols], X[:, cols], bank[1][:, :], ALU.add).then_inc(S["x1_done"], 1)
                    wait(dve, "x1_done", c - 1)
                    stats(1, c - 2)
                if has(c):
                    wait(dve, "landed", c + 1)
                    stats(0, c)
                if has(c, 2):
                    wait(dve, "sqrt2", c - 1)
                    V.reciprocal(rs[:, 1, bass.ts(c - 2, TPC)], sd[:, 1, bass.ts(c - 2, TPC)]).then_inc(S["recip2"], 1)
                if has(c):
                    wait(dve, "s_done", c + 1)
                    wait(dve, "o_done", c)
                    V.tensor_tensor(tile4(sm), tile4(bank[0][:, :]), cm[:, :].rearrange("p (a n) -> p a n", a=1)
                                    .broadcast_to([P, TPC, P]), ALU.mult).then_inc(S["sm_done"], 1)
                    wait(dve, "sqrt1", c + 1)
                    V.reciprocal(rs[:, 0, bass.ts(c, TPC)], sd[:, 0, bass.ts(c, TPC)]).then_inc(S["recip1"], 1)
                    wait(dve, "recip1", c + 1)
                    V.scalar_tensor_tensor(nb1[:, bass.ts(c, TPC)], mv[0][:, bass.ts(c, TPC), 0], -1.0,
                                           rs[:, 0, bass.ts(c, TPC)], ALU.mult, ALU.mult).then_inc(S["nb1_done"], 1)

            skewed(dve, stage_a, 3)

            count = [0]

            def link(instruction):
                count[0] += 1
                instruction.then_inc(S["route"], 1)
                dve.wait_ge(S["route"], count[0])

            def by_expert(ap):
                return ap.rearrange("p (t e) -> p t e", e=E)

            def per_tile(ap):
                return ap.rearrange("p (t a) -> p t a", a=1).broadcast_to([P, NT, E])

            dve.wait_ge(S["logits_done"], NCH)
            dve.wait_ge(S["wprep_done"], 1)
            dve.wait_ge(S["b3_ready"], 1)
            link(V.tensor_reduce(g_m, logits, AX.X, ALU.max))
            V.tensor_tensor(by_expert(g_a), logits, per_tile(g_m), ALU.subtract).then_inc(S["shifted"], 1)
            dve.wait_ge(S["exp_g"], 1)
            link(V.tensor_reduce(g_r, by_expert(g_sc), AX.X, ALU.add))
            link(V.reciprocal(g_m, g_r))
            link(V.tensor_tensor(by_expert(g_sc), by_expert(g_sc), per_tile(g_m), ALU.mult))
            last_of = {}
            for src, hot in ((g_sc, g_b), (g_a, g_c)):
                link(V.tensor_reduce(g_m, by_expert(src), AX.X, ALU.max))
                link(V.tensor_tensor(by_expert(hot), by_expert(src), per_tile(g_m), ALU.is_equal))
                link(V.tensor_tensor(by_expert(hot), by_expert(hot), d8[:, :].rearrange("p (a e) -> p a e", a=1)
                                     .broadcast_to([P, NT, E]), ALU.mult))
                link(V.tensor_reduce(g_m, by_expert(hot), AX.X, ALU.max))
                link(V.tensor_tensor(by_expert(hot), by_expert(hot), per_tile(g_m), ALU.is_equal))
                if hot is g_b:
                    link(V.scalar_tensor_tensor(g_a, g_b, -2.0, g_sc, ALU.mult, ALU.add))
            link(V.tensor_tensor(g_b, g_b, g_c, ALU.add))
            V.tensor_tensor(g_a, g_sc, g_b, ALU.mult).then_inc(S["routed_w"], 1)
            V.tensor_copy(g_mask, g_b).then_inc(S["routed_m"], 1)
            dve.wait_ge(S["expclip"], 1)
            link(V.tensor_scalar(sig[:, :], sig[:, :], 1.0, None, ALU.add))
            link(V.reciprocal(sig[:, :], sig[:, :]))

            def stage_b(c, e):
                n = E * c + e
                here = has(c)
                if here:
                    half = e // 4
                    wait(dve, f"wb_dma{half}", 16 * (c + 1))
                    wait(dve, "xh_done", n - 1)
                    wait(dve, "xl_done", n - 1)
                    V.tensor_tensor(tile4(bank[e % 2][:, :]), tile4(n2_t[:, bass.ts(c, CH)]),
                                    wb[:, half, :, e % 4 * P:(e % 4 + 1) * P], ALU.mult).then_inc(S["xs_done"], 1)
                if step_exists(c, e, 1):
                    k = (e - 1) % E
                    wait(dve, "xh_done", n)
                    wait(dve, "p3_done", n - 2)
                    V.tensor_tensor(xl[:, k % 2, :], bank[k % 2][:, :], xh[:, k % 2, :].bitcast(fp32), ALU.subtract)\
                        .then_inc(S["xl_done"], 1)
                if here and e == 0:
                    wait(dve, "nh_done", c + 1)
                    wait(dve, "ab_done", 2 * c)
                    V.tensor_tensor(nl[:, :], n2_t[:, bass.ts(c, CH)], nh[:, :].bitcast(fp32), ALU.subtract)\
                        .then_inc(S["nl_done"], 1)
                if step_exists(c, e, 4):
                    k = (e - 4) % E
                    wait(dve, "p2_done", n - 3)
                    wait(dve, "m3_done", n - 3)
                    wait(dve, "acc_done", n - 5)
                    V.scalar_tensor_tensor(prod[:, k % 2, :], bank[5][:, :], bias[:, 8 + k:9 + k], m3[:, k % 4, :],
                                           ALU.add, ALU.mult).then_inc(S["prod_done"], 1)
                if here and e in (1, 3):
                    i = e // 2
                    wait(dve, "ga_done", 2 * c + i + 1)
                    wait(dve, "gl_done", 2 * c + i)
                    V.tensor_tensor(gg, bank[7][:, :], ga, ALU.mult).then_inc(S["g_done"], 1)
                    wait(dve, "g_done", 2 * c + i + 1)
                    wait(dve, "z_done", c)
                    V.tensor_copy(gh[:, i, :], gg).then_inc(S["gh_done"], 1)
                    wait(dve, "gh_done", 2 * c + i + 1)
                    V.tensor_tensor(gl[:, i, :], gg, gh[:, i, :].bitcast(fp32), ALU.subtract).then_inc(S["gl_done"], 1)
                if e == 7 and has(c, 1):
                    wait(dve, "yt_done", c + 1)
                    cols = bass.ts(c - 1, CH)
                    V.tensor_tensor(X[:, cols], X[:, cols], bank[7][:, :], ALU.add).then_inc(S["x2_done"], 1)
                    wait(dve, "x2_done", c + 1)
                    stats(2, c - 1)

            steps(dve, stage_b)

            dve.wait_ge(S["sqrt3"], 1)
            V.reciprocal(rs[:, 2, :], sd[:, 2, :]).then_inc(S["recip3"], 1)

            def stage_c(c):
                if has(c):
                    wait(dve, "sc_pe", c + 1)
                    raw = bank[5][:, 0:TPC * SEQ].rearrange("p (t k) -> p t k", t=TPC)
                    V.tensor_reduce(mx[:, :], raw, AX.X, ALU.max).then_inc(S["max_done"], 1)
                    wait(dve, "max_done", c + 1)
                    wait(dve, "exp_done", 2 * c)
                    V.tensor_tensor(sc, raw, mx[:, :].rearrange("p (t a) -> p t a", a=1).broadcast_to([P, TPC, SEQ]),
                                    ALU.subtract).then_inc(S["sub_done"], 1)
                if has(c, 1):
                    wait(dve, "o3_pe", c)
                    wait(dve, "rinv_done", c)
                    for t in range(TPC):
                        x_tile = X[:, bass.ds((c - 1) * CH + t * P, P)]
                        last = V.scalar_tensor_tensor(x_tile, bank[6][:, t * P:(t + 1) * P], rinv[:, t:t + 1], x_tile,
                                                      ALU.mult, ALU.add)
                    last.then_inc(S["x3_done"], 1)
                    wait(dve, "x3_done", c)
                    stats(3, c - 1)
                if has(c):
                    wait(dve, "exp_done", 2 * (c + 1))
                    V.tensor_reduce(rsum[:, :], pr, AX.X, ALU.add).then_inc(S["sum_done"], 1)
                    wait(dve, "sum_done", c + 1)
                    V.reciprocal(rinv[:, :], rsum[:, :]).then_inc(S["rinv_done"], 1)

            skewed(dve, stage_c, 2)

            dve.wait_ge(S["sqrt4"], 1)
            V.reciprocal(rs[:, 3, :], sd[:, 3, :]).then_inc(S["recip4"], 1)
            dve.wait_ge(S["recip4"], 1)
            V.scalar_tensor_tensor(nb4[:, :], mv[3][:, :, 0], -1.0, rs[:, 3, :], ALU.mult, ALU.mult).then_inc(S["nb4_done"], 1)
            dve.wait_ge(S["nb4_done"], 1)
            with dve.Fori(0, NCH) as c:
                for t in range(2, TPC):
                    j = c * TPC + t
                    last = V.tensor_scalar(arena[:, bass.ds(c * 3 * CH + t * P, P)], X[:, bass.ts(j, P)],
                                           rs[:, 3, bass.ds(j, 1)], nb4[:, bass.ds(j, 1)], ALU.mult, ALU.add)
                last.then_inc(S["n4_dve"], 1)
                wait(dve, "n4_act", c + 1)
                wait(dve, "n4_dve", c + 1)
                V.tensor_reduce(am[:, 0, bass.ds(c, 1)], arena[:, bass.ds(c * 3 * CH, CH)], AX.X, ALU.max,
                                apply_absolute_value=True).then_inc(S["am_done"], 1)

            def quant_scale(j, last_max, value):
                first = j * 6
                dve.wait_ge(S[last_max], value)
                V.tensor_reduce(qs[:, j, 0:1], am[:, j, :], AX.X, ALU.max).then_inc(S["qs_step"], 1)
                dve.wait_ge(S["qs_all"], j + 1)
                V.scalar_tensor_tensor(qs[:, j, 2:3], qs[:, j, 1:2], 1.0 / QMAX, sig[:, j:j + 1], ALU.mult, ALU.mult)\
                    .then_inc(S["qs_step"], 1)
                dve.wait_ge(S["qs_step"], first + 2)
                V.reciprocal(qs[:, j, 3:4], qs[:, j, 2:3]).then_inc(S["qs_step"], 1)
                V.tensor_scalar(qs[:, j, 4:5], qs[:, j, 2:3], -QMAX - 1.0, None, ALU.mult).then_inc(S["qs_step"], 1)
                V.tensor_scalar(qs[:, j, 5:6], qs[:, j, 2:3], QMAX, None, ALU.mult).then_inc(S["qs_step"], 1)
                if j == 0:
                    V.tensor_scalar(wgu_i[:, 0:6], wgu_s[:, 0:6], qs[:, 0, 2:3], None, ALU.mult).then_inc(S["qs_step"], 1)
                else:
                    V.tensor_scalar(down_scale[:, :], down_scale[:, :], qs[:, 1, 2:3], None, ALU.mult)\
                        .then_inc(S["qs_step"], 1)
                dve.wait_ge(S["qs_step"], first + 6)
                dve.sem_inc(S["qs_dve"], 1)

            quant_scale(0, "am_done", NCH)

            def stage_d2(c):
                if has(c):
                    first = arena[:, bass.ds(c * 3 * CH, CH)]
                    V.tensor_scalar(first, first, qs[:, 0, 4:5], qs[:, 0, 5:6], ALU.max, ALU.min).then_inc(S["clamp_done"], 1)
                if has(c, 1):
                    for b in range(NB_FFN):
                        wait(dve, "sg_done", 3 * (c - 1) + b + 1)
                        V.scalar_tensor_tensor(arena[:, bass.ds((c - 1) * 3 * CH + b * CH, CH)], bank[4 + b][:, :],
                                               wgu_i[:, 3 + b:4 + b], sg[:, b * CH:(b + 1) * CH], ALU.mult, ALU.mult)\
                            .then_inc(S["h_done"], 1)
                if has(c):
                    wait(dve, "t4_done", c + 1)
                    wait(dve, "gu_done", 3 * c)
                    V.tensor_scalar(xq[:, :], bank[0][:, :], MAGIC, None, ALU.subtract).then_inc(S["xq_done"], 1)
                if has(c, 1):
                    wait(dve, "h_done", 3 * c)
                    V.tensor_reduce(am[:, 1, bass.ds(c - 1, 1)], arena[:, bass.ds((c - 1) * 3 * CH, 3 * CH)], AX.X, ALU.max,
                                    apply_absolute_value=True).then_inc(S["hmax_done"], 1)

            skewed(dve, stage_d2, 1)
            quant_scale(1, "hmax_done", NCH)

            def stage_d3(c):
                if has(c):
                    hid = arena[:, bass.ds(c * 3 * CH, 3 * CH)]
                    V.tensor_scalar(hid, hid, qs[:, 1, 4:5], qs[:, 1, 5:6], ALU.max, ALU.min).then_inc(S["hclamp_done"], 1)
                if has(c, 1):
                    wait(dve, "hmagic_done", c)
                    wait(dve, "down_done", c - 1)
                    V.tensor_scalar(hq, arena[:, bass.ds((c - 1) * 3 * CH, 3 * CH)], MAGIC, None, ALU.subtract)\
                        .then_inc(S["hq_done"], 1)
                if has(c, 2):
                    wait(dve, "down_done", c - 1)
                    wait(dve, "added_done", c - 2)
                    V.tensor_tensor(tile4(scaled[:, 0, :]), tile4(bank[7][:, :]),
                                    down_scale[:, :].rearrange("p (a n) -> p a n", a=1).broadcast_to([P, TPC, P]),
                                    ALU.mult).then_inc(S["scaled_done"], 1)

            skewed(dve, stage_d3, 3)

        @block.gpsimd
        def _(pool):
            G = nc.gpsimd

            G.memset(eps_t[:, :], EPS)
            G.memset(magic_t[:, :], MAGIC)
            G.memset(ones[:, :], 1.0)
            G.memset(mk[:, :], 0.0)
            G.memset(b3s[:, :, :], 0.0)
            pool.wait_ge(S["consts"], 48)
            G.tensor_copy(id16[:, :], id32[:, :]).then_inc(S["pool_consts"], 1)
            pool.wait_ge(S["pool_consts"], 1)

            count = [0]

            def link(instruction):
                count[0] += 1
                instruction.then_inc(S["b3_step"], 1)
                pool.wait_ge(S["b3_step"], count[0])

            pool.wait_ge(S["small_dma"], 144)
            link(G.tensor_copy(b3h[:, :], b3a))
            link(G.tensor_tensor(b3b, b3a, b3h[:, :], ALU.subtract))
            link(G.tensor_scalar(b3c, b3h[:, :], pick[:, 0:1], None, ALU.mult))
            for part in (1, 2):
                link(G.tensor_copy(b3h[:, :], b3b))
                link(G.tensor_tensor(b3b, b3b, b3h[:, :], ALU.subtract))
                link(G.tensor_scalar(b3a, b3h[:, :], pick[:, part:part + 1], None, ALU.mult))
                link(G.tensor_tensor(b3c, b3c, b3a, ALU.add))
            for e in range(E):
                last = G.tensor_scalar(b3s[0:24, e, :], b3c, pick[:, 3 + e:4 + e], None, ALU.mult)
            last.then_inc(S["b3_ready"], 1)

            def normalise(dst, norm, c, done):
                tiles = bass.ts(c, TPC)
                mean = mv[norm][:, tiles, 0:1].broadcast_to([P, TPC, P])
                inverse = rs[:, norm, tiles].rearrange("p (t a) -> p t a", a=1).broadcast_to([P, TPC, P])
                centred = f"centred{norm}"
                G.tensor_tensor(tile4(dst), tile4(X[:, bass.ts(c, CH)]), mean, ALU.subtract).then_inc(S[centred], 1)
                pool.wait_ge(S[centred], c + 1)
                G.tensor_tensor(tile4(dst), tile4(dst), inverse, ALU.mult).then_inc(S[done], 1)

            def stage_a(c):
                if has(c, 2):
                    wait(pool, "recip2", c - 1)
                    wait(pool, "t2_done", c - 2)
                    normalise(n2, 1, c - 2, "n2_done")
                if has(c):
                    wait(pool, "xn_done", c + 1)
                    cols = bass.ts(c, CH)
                    G.tensor_tensor(X[:, cols], X[:, cols], xn, ALU.add).then_inc(S["base_done"], 1)

            skewed(pool, stage_a, 3)
            pool.wait_ge(S["wh_done"], 1)
            G.tensor_tensor(wl[:, :, :], wstage, wh[:, :, :].bitcast(fp32), ALU.subtract).then_inc(S["wl_done"], 1)

            def stage_b(c, e):
                n = E * c + e
                if step_exists(c, e, 1):
                    k = (e - 1) % E
                    wait(pool, "silu_done", n)
                    wait(pool, "hh_done", n)
                    wait(pool, "p2_done", n - 4)
                    G.tensor_tensor(hl[:, k % 4, :], h_sb[:, k % 2, :], hh[:, k % 4, :].bitcast(fp32), ALU.subtract)\
                        .then_inc(S["hl_done"], 1)
                if step_exists(c, e, 5):
                    k = (e - 5) % E
                    chunk = c if e >= 5 else c - 1
                    wait(pool, "prod_done", n - 4)
                    wait(pool, "acc_done", n - 5)
                    if k == 0:
                        wait(pool, "zz_done", chunk + 1)
                    if k == 7:
                        wait(pool, "yt_done", chunk + 1)
                    G.tensor_tensor(yf if k == 7 else yy, zz if k == 0 else yy, prod[:, k % 2, :], ALU.add)\
                        .then_inc(S["acc_done"], 1)

            steps(pool, stage_b)

            pool.wait_ge(S["x2_done"], NCH + 1)
            pool.wait_ge(S["xl_done"], E * NCH)
            pool.wait_ge(S["nh_done"], NCH)
            G.memset(pr, 0.0).then_inc(S["pr_zero"], 1)
            pool.wait_ge(S["recip3"], 1)

            def stage_c(c):
                wait(pool, "t3_done", c)
                normalise(n3, 2, c, "n3_done")

            stage_c(0)
            with pool.Fori(1, NCH) as c:
                stage_c(c)

            for j in range(2):
                pool.wait_ge(S["qs_step"], 6 * j + 1)
                G.partition_all_reduce(qs[:, j, 1:2], qs[:, j, 0:1], P, RMAX).then_inc(S["qs_all"], 1)
            with pool.Fori(0, NCH) as c:
                wait(pool, "scaled_done", c + 1)
                cols = bass.ts(c, CH)
                G.tensor_tensor(X[:, cols], X[:, cols], scaled[:, 0, :], ALU.add).then_inc(S["added_done"], 1)


def step_exists(c, e, lag):
    return not isinstance(c, int) or 0 <= E * c + e - lag < E * NCH


def steps(engine, step):
    for e in range(E):
        step(0, e)
    with engine.Fori(1, NCH) as c:
        for e in range(E):
            step(c, e)
    for e in range(E):
        step(NCH, e)


def kernel(x, ctx_1024, L0_ffn_gate_w, L0_ffn_w1, L0_ffn_b1, L0_ffn_w2, L0_ffn_b2, L0_ffn_w3, L0_ffn_b3, L0_ffn_sw1,
           L0_ffn_sw2, L0_ffn_sw3, L1_xattn_Wq, L1_xattn_bq, L1_xattn_qk_b, L1_xattn_Wv, L1_xattn_bv, L1_ffn_clip_x,
           L1_ffn_clip_down, L1_ffn_w_gate, L1_ffn_w_up, L1_ffn_w_down):
    import numpy as np
    import concourse.bacc as bacc
    from concourse.bass_utils import run_bass_kernel_spmd

    f32 = np.float32
    ctx2 = np.ascontiguousarray(np.asarray(ctx_1024).reshape(TOK, P).T)
    blocks = [L0_ffn_w1[e].T for e in range(E)] + [L0_ffn_w3[e].T for e in range(E)] + [L0_ffn_w2[e].T for e in range(E)]
    blocks += [L0_ffn_sw1[i * P:(i + 1) * P].T for i in range(2)] + [L0_ffn_sw2[i * P:(i + 1) * P].T for i in range(2)]
    blocks += [L0_ffn_sw3[:, i * P:(i + 1) * P].T for i in range(2)]
    wall = np.concatenate([np.asarray(b) for b in blocks], axis=1)
    biases = np.concatenate([np.asarray(a) for a in (L0_ffn_b1.T, L0_ffn_b2.T, L1_xattn_bq[:, None],
                                                     L1_xattn_qk_b[:, None], L1_xattn_bv[:, None])], axis=1)
    wgu = np.zeros((P, 2 * NB_FFN, P), f32)
    for j, w in enumerate((L1_ffn_w_gate, L1_ffn_w_up)):
        for b in range(NB_FFN):
            rows = np.asarray(w[b * P:min((b + 1) * P, I_FFN)])
            wgu[:rows.shape[0], j * NB_FFN + b, :] = rows
    wd = np.zeros((P, NB_FFN * P), f32)
    wd[:, :I_FFN] = np.asarray(L1_ffn_w_down)
    ident = np.eye(P, dtype=f32)
    s, t = np.arange(P)[:, None], np.arange(P)[None, :]
    causal = ((s // SEQ == t // SEQ) & (s <= t)).astype(f32)
    down8 = np.tile(np.arange(E, 0, -1, dtype=f32), (P, 1))
    pick = np.zeros((3 * E, 3 + E), f32)
    for r in range(3 * E):
        pick[r, r // E] = 1.0
        pick[r, 3 + r % E] = 1.0
    ins = dict(
        x=np.asarray(x).reshape(TOK, P), ctxT=ctx2, wall=wall, biases=biases,
        b3rep=np.concatenate([np.asarray(L0_ffn_b3)] * 3, axis=0), b3pick=pick, gateT=np.asarray(L0_ffn_gate_w).T,
        wqT=np.asarray(L1_xattn_Wq).T, wvT=np.asarray(L1_xattn_Wv).T, wgu=wgu.reshape(P, -1), wd=wd,
        clips=np.concatenate([np.asarray(L1_ffn_clip_x), np.asarray(L1_ffn_clip_down)]), ident=ident, causal=causal,
        down8=down8)
    ins = {k: np.ascontiguousarray(v) for k, v in ins.items()}
    nc = bacc.Bacc("TRN2", target_bir_lowering=False, num_devices=1, dynamic_dma_scratch_size=1024)
    args = {k: nc.dram_tensor(f"in_{k}", v.shape, mybir.dt.from_np(v.dtype), kind="ExternalInput").ap() for k, v in ins.items()}
    args["out"] = nc.dram_tensor("out", (TOK, P), fp32, kind="ExternalOutput").ap()
    build(nc, **args)
    r = run_bass_kernel_spmd(nc, [{f"in_{k}": v for k, v in ins.items()}], core_ids=[0])
    return np.asarray(r.results[0]["out"]).reshape(P, SEQ, P)
```

```python
from contextlib import ExitStack

import concourse.bass as bass
from concourse import mybir

fp32 = mybir.dt.float32
fp32r = mybir.dt.float32r
bf16 = mybir.dt.bfloat16
i32 = mybir.dt.int32
ALU = mybir.AluOpType
ACT = mybir.ActivationFunctionType
AX = mybir.AxisListType
RMAX = bass.bass_isa.ReduceOp.max

P = 128
TOK = 8192
SEQ = 64
CH = 512
TPC = CH // P
NCH = TOK // CH
NT = TOK // P
E = 8
NB_FFN = 3
I_FFN = 352
EPS = 1e-5
QMAX = 127.0
MAGIC = 12582912.0
W1, W3, SW1, SW2 = 0, 8, 16, 18
NW = 20
W2, SW3 = 0, 8
NF = 10
SCORE_SCALE = (P / 16) ** -0.5


def build(nc, x, ctxT, wall, wfull, biases, b3rep, b3pick, gateT, wqT, wvT, wgu, wd, clips, ident, causal, down8, out):
    x_v = x.rearrange("(t p) d -> p t d", p=P)
    out_v = out.rearrange("(t p) d -> p t d", p=P)
    weight_dram = nc.dram_tensor("weight_by_tile", (NT * E, P), fp32).ap()
    mask_dram = nc.dram_tensor("mask_by_tile", (NT * E, P), bf16).ap()

    with ExitStack() as ctx:
        def sb(name, shape, dt=fp32):
            return ctx.enter_context(nc.sbuf_tensor(name, shape, dt))

        def sem(name):
            return ctx.enter_context(nc.semaphore(name))

        X = sb("X", [P, TOK])
        arena = sb("arena", [P, 3 * TOK])
        ctx_t = arena[:, 0:TOK]
        n2_t = arena[:, TOK:2 * TOK]
        misc = arena[:, 2 * TOK:3 * TOK]
        ctx_now = misc[:, 0:512]
        sm = misc[:, 512:1024]
        xn = misc[:, 1024:1536]
        n2 = misc[:, 1536:2048]
        n2_now = misc[:, 2048:2560]
        wstage = misc[:, 3072:3072 + NW * P].rearrange("p (b n) -> p b n", n=P)
        cm = misc[:, 7168:7296]
        ones = misc[:, 7296:7424]
        g_tr = misc[:, 0:512]
        g_mtr = misc[:, 512:768].bitcast(bf16)
        wb = misc[:, 0:4096].rearrange("p (h t n) -> p h t n", h=2, t=TPC)
        m3 = misc[:, 4096:6144].rearrange("p (b n) -> p b n", b=4)
        prod = misc[:, 6144:8192].rearrange("p (b n) -> p b n", b=4)
        n3 = n2_t[:, 0:512]
        n3_t = n2_t[:, 512:1024]
        q_t = n2_t[:, 1024:1536]
        v_t = n2_t[:, 1536:2048]
        v_tok = n2_t[:, 2048:2560]
        sc = n2_t[:, 2560:2816].rearrange("p (t k) -> p t k", t=TPC)
        pr = n2_t[:, 3072:3584].rearrange("p (t k) -> p t k", t=TPC)
        pr_t = n2_t[:, 3584:4096]
        wq = n2_t[:, 4096:4224]
        wv = n2_t[:, 4224:4352]

        wh = sb("wh", [P, NW, P], fp32r)
        wl = sb("wl", [P, NW, P], fp32r)
        nh = sb("nh", [P, CH], fp32r)
        nl = sb("nl", [P, CH], fp32r)
        xh = sb("xh", [P, 4, CH], fp32r)
        xl = sb("xl", [P, 4, CH], fp32r)
        wf = sb("wf", [P, NF, P])
        xs = sb("xs", [P, 4, CH])
        hid_b = sb("hid_b", [P, 4, CH])
        gg = sb("gg", [P, 2, CH])
        work = sb("work", [P, 5 * CH])
        ga, zz, yy, yf = (work[:, i * CH:(i + 1) * CH] for i in range(4))
        wgu_f = work[:, 0:768].rearrange("p (b n) -> p b n", n=P)
        wd_f = work[:, 768:1152]
        wgu_q = work[:, 1152:1536].bitcast(bf16)
        wd_q = work[:, 1536:1728].bitcast(bf16)
        wd_diag = work[:, 1792:1920]
        b3a = work[0:24, 1920:2048]
        b3b = work[0:24, 2048:2176]
        b3c = work[0:24, 2176:2304]
        b3h = work[0:24, 2304:2368].bitcast(bf16)
        g_sc, g_a, g_b, g_c = (work[:, i * CH:(i + 1) * CH] for i in range(4))
        g_mask = work[:, 2048:2304].bitcast(bf16)
        g_m = work[:, 2304:2368]
        g_r = work[:, 2368:2432]
        qn = work[:, 0:512]
        sg = work[:, 512:2048]
        xq = work[:, 2048:2304].bitcast(bf16)
        hq = work[:, 0:768].bitcast(bf16)
        scaled = work[:, 1024:2048].rearrange("p (b n) -> p b n", b=2)

        mk = sb("mk", [P, 2 * CH], bf16)
        b3s = sb("b3s", [P, E, P], bf16)
        pick = sb("pick", [24, 3 + E])
        bias = sb("bias", [P, 19])
        bqk = sb("bqk", [P, 1])
        gate_w = sb("gate_w", [P, E])
        wgq = sb("wgq", [P, 2 * NB_FFN * P], bf16)
        wdq = sb("wdq", [P, NB_FFN * P], bf16)
        wgu_s = sb("wgu_s", [P, 8])
        wgu_i = sb("wgu_i", [P, 8])
        down_scale = sb("down_scale", [P, P])
        id32 = sb("id32", [P, P])
        id16 = sb("id16", [P, P], bf16)
        d8 = sb("d8", [P, E])
        eps_t = sb("eps_t", [P, 1])
        magic_t = sb("magic_t", [P, 1])
        clip = sb("clip", [P, 2])
        sig = sb("sig", [P, 2])
        stat = sb("stat", [P, 2, TPC, 6])
        mv = [sb(f"mv{i}", [P, NT, 2]) for i in range(2)] * 2
        sd = [sb(f"sd{i}", [P, NT]) for i in range(2)] * 2
        rs = [sb(f"rs{i}", [P, NT]) for i in range(2)] * 2
        mv_now = sb("mv_now", [P, 2, TPC, 2])
        nb1 = nb4 = sb("nb", [P, NT])
        mx = sb("mx", [P, TPC])
        rsum = sb("rsum", [P, TPC])
        rinv = sb("rinv", [P, TPC])
        am = sb("am", [P, 2, NCH])
        qs = sb("qs", [P, 2, 8])

        bank = [ctx.enter_context(nc.psum_tensor(f"bank{i}", [P, CH], fp32)) for i in range(8)]
        bank16 = [b[:, :].bitcast(bf16)[:, 0:CH] for b in bank]
        p1_bank = bank[2][:, :], bank[3][:, :]
        p2_bank = bank[1][:, :], bank[5][:, :]
        p3_bank = bank[0][:, :], bank[4][:, :]
        logits = bank[3][:, :].rearrange("p (t e) -> p t e", e=E)

        LOADS = [(0, 1), (1, 1), (2, 2), (4, 4), (8, 8)]
        x_dma = [sem(f"x_dma{i}") for i in range(len(LOADS))]
        c_dma = [sem(f"c_dma{i}") for i in range(len(LOADS))]
        names = """consts weights_dma small_dma landed pool_consts
            amax_done wscale_done wgu_rounded wd_rounded diag_done wprep_pe wprep_done bqk_done b3_step b3_ready
            stat1_done stats1 sqrt1 recip1 xn_done base_done ctx_copied s_done sm_done o_done x1_done stat2_done stats2
            sqrt2 recip2 n2_done t2_done n2_copied n2_stored logits_done wh_done wl_done
            route shifted exp_g expclip routed_w routed_m route_t_w route_t_m trw_copied trm_copied
            weight_stored mask_stored
            wb_dma0 wb_dma1 mk_dma nh_done nl_done xs_done xh_done xl_done p1_done p3_done p2_done
            silu_done zz_added m3_done prod_done acc_done ab_done ga_done g_done z_done
            zz_done yt_done x2_done stat3_done stats3 sqrt3 recip3 pr_zero
            n3_done t3_done n3t_done vt_pe vt_done qt_pe qt_done v_pe v_done sc_pe max_done sub_done exp_done
            sum_done rinv_done pt_pe pt_done o3_pe x3_done stat4_done stats4 sqrt4 recip4 nb4_done
            n4_act am_done qs_step qs_dve qs_all clamp_done magic_done t4_done xq_done gu_done sg_done
            h_done hmax_done hclamp_done hmagic_done hq_done down_done scaled_done added_done out_dma c_weights sp_held dve_held aggr1_done aggr2_done aggr3_done aggr4_done nb1_done centred1 centred2 n4_dve""".split()
        S = {n: sem(n) for n in names}

        def has(c, lag=0):
            return not isinstance(c, int) or 0 <= c - lag < NCH

        def skewed(engine, slot, lag):
            for c in range(lag):
                slot(c)
            with engine.Fori(lag, NCH) as c:
                slot(c)
            for c in range(NCH, NCH + lag):
                slot(c)

        def wait(engine, name, value):
            if not isinstance(value, int) or value > 0:
                engine.wait_ge(S[name], value)

        def tile4(ap):
            return ap.rearrange("p (t n) -> p t n", t=TPC)

        block = ctx.enter_context(nc.Block())

        @block.sync
        def _(sp):
            for dst, src in ((id32, ident), (cm, causal), (gate_w, gateT)):
                sp.dma_start(dst[:, :], src).then_inc(S["consts"], 16)
            for i, (c0, n) in enumerate(LOADS):
                sp.dma_start(X[:, c0 * CH:(c0 + n) * CH].rearrange("p (t d) -> p t d", d=P),
                             x_v[:, c0 * TPC:(c0 + n) * TPC, :]).then_inc(x_dma[i], 16)
                sp.dma_start(ctx_t[:, c0 * CH:(c0 + n) * CH], ctxT[:, c0 * CH:(c0 + n) * CH]).then_inc(c_dma[i], 16)
                if i == 0:
                    small = ((work[:, 0:768], wgu), (wd_f, wd), (bias[:, :], biases),
                             (d8[:, :], down8), (b3a, b3rep), (pick[:, :], b3pick), (clip[:, :], clips.partition_broadcast(P)))
                    for dst, src in small:
                        sp.dma_start(dst, src).then_inc(S["small_dma"], 16)
            sp.dma_start(misc[:, 3072:3072 + NW * P], wall).then_inc(S["weights_dma"], 16)
            sp.dma_start(wf[:, :, :].rearrange("p b n -> p (b n)"), wfull).then_inc(S["weights_dma"], 16)
            sp.wait_ge(S["consts"], 48)
            for i, (c0, n) in enumerate(LOADS):
                sp.wait_ge(x_dma[i], 16)
                sp.wait_ge(c_dma[i], 16)
                sp.sem_inc(S["landed"], n)
            for g in range(4):
                cols = slice(g * P, (g + 1) * P)
                sp.wait_ge(S["trw_copied"], 1)
                sp.dma_start(weight_dram[cols, :], g_tr[:, cols]).then_inc(S["weight_stored"], 16)
                sp.wait_ge(S["trm_copied"], 1)
                sp.dma_start(mask_dram[cols, :], g_mtr[:, cols]).then_inc(S["mask_stored"], 16)
            sp.wait_ge(S["weight_stored"], 64)
            sp.wait_ge(S["mask_stored"], 64)

            w_v = weight_dram.rearrange("(c t e) k -> c t (e k)", t=TPC, e=E)
            k_v = mask_dram.rearrange("(c t e) k -> c e t k", t=TPC, e=E)

            def broadcast(c, half):
                src = w_v[bass.ds(c, 1), :, half * 512:half * 512 + 512]
                src = src.rearrange("c t n -> (c t) n").partition_broadcast(P)
                sp.dma_start(wb[:, half, :, :], src).then_inc(S[f"wb_dma{half}"], 16)

            def masks(c):
                for part in range(3):
                    dst = mk[part * E:(part + 1) * E, bass.ds((c % 2) * CH, CH)].rearrange("e (t k) -> e t k", t=TPC)
                    src = k_v[bass.ds(c, 1), :, :, :].rearrange("c e t k -> (c e) t k")
                    sp.dma_start(dst, src).then_inc(S["mk_dma"], 16)

            sp.wait_ge(S["pool_consts"], 1)
            masks(0)
            sp.wait_ge(S["wl_done"], 1)
            sp.wait_ge(S["wh_done"], 1)
            sp.wait_ge(S["logits_done"], NCH)
            broadcast(0, 0)
            broadcast(0, 1)
            sp.wait_ge(S["mk_dma"], 48)
            masks(1)

            def hold(name, value):
                sp.wait_ge(S[name], value)
                sp.sem_inc(S["sp_held"], 1)

            def next_chunk(c):
                hold("xs_done", E * c - 4)
                broadcast(c, 0)
                hold("xs_done", E * c)
                broadcast(c, 1)

            next_chunk(1)
            with sp.Fori(2, NCH) as c:
                hold("mk_dma", 48 * c)
                hold("p3_done", E * (c - 1))
                masks(c)
                next_chunk(c)

            sp.wait_ge(S["nl_done"], NCH)
            sp.wait_ge(S["xs_done"], E * NCH)
            sp.dma_start(wq, wqT).then_inc(S["c_weights"], 16)
            sp.dma_start(wv, wvT).then_inc(S["c_weights"], 16)

            with sp.Fori(0, NCH) as c:
                hold("added_done", c + 1)
                sp.dma_start(out_v[:, bass.ts(c, TPC), :], X[:, bass.ts(c, CH)].rearrange("p (t d) -> p t d", d=P))\
                    .then_inc(S["out_dma"], 16)
            sp.wait_ge(S["out_dma"], 16 * NCH)

        @block.tensor
        def _(pe):
            mm = nc.tensor.matmul
            pe.sem_inc(S["yt_done"], 1)

            pe.wait_ge(S["consts"], 48)
            pe.wait_ge(S["pool_consts"], 1)
            pe.wait_ge(S["wgu_rounded"], 1)
            for b in range(2 * NB_FFN):
                nc.tensor.transpose(bank16[4 + b // 4][:, b % 4 * P:(b % 4 + 1) * P], wgu_q[:, b * P:(b + 1) * P], id16[:, :])
            pe.wait_ge(S["wd_rounded"], 1)
            for b in range(NB_FFN):
                nc.tensor.transpose(bank16[6][:, b * P:(b + 1) * P], wd_q[:, b * P:(b + 1) * P], id16[:, :])
            pe.wait_ge(S["diag_done"], 1)
            mm(bank[7][:, 0:P], ones[:, :], wd_diag, start=True, stop=True).then_inc(S["wprep_pe"], 1)

            def stage_a(c):
                if has(c):
                    wait(pe, "ctx_copied", c + 1)
                    wait(pe, "sm_done", c)
                    for t in range(TPC):
                        tile = ctx_now[:, t * P:(t + 1) * P]
                        last = mm(bank[0][:, t * P:(t + 1) * P], tile, tile, start=True, stop=True)
                    last.then_inc(S["s_done"], 1)
                if has(c, 1):
                    wait(pe, "sm_done", c)
                    wait(pe, "xn_done", c)
                    wait(pe, "x1_done", c - 1)
                    for t in range(TPC):
                        cols = slice(t * P, (t + 1) * P)
                        last = mm(bank[1][:, cols], sm[:, cols], xn[:, cols], start=True, stop=True)
                    last.then_inc(S["o_done"], 1)
                if has(c, 2):
                    wait(pe, "n2_done", c - 1)
                    wait(pe, "n2_stored", c - 2)
                    for t in range(TPC):
                        cols = slice(t * P, (t + 1) * P)
                        last = nc.tensor.transpose(bank[2][:, cols], n2[:, cols], id32[:, :])
                    last.then_inc(S["t2_done"], 1)
                if has(c, 3):
                    wait(pe, "n2_copied", c - 2)
                    for t in range(TPC):
                        last = mm(bank[3][:, bass.ds(((c - 3) * TPC + t) * E, E)], n2_now[:, t * P:(t + 1) * P],
                                  gate_w[:, :], start=True, stop=True)
                    last.then_inc(S["logits_done"], 1)

            skewed(pe, stage_a, 3)

            pe.wait_ge(S["routed_w"], 1)
            for g in range(4):
                last = nc.tensor.transpose(bank[0][:, g * P:(g + 1) * P], g_a[:, g * P:(g + 1) * P], id32[:, :])
            last.then_inc(S["route_t_w"], 1)
            pe.wait_ge(S["routed_m"], 1)
            for g in range(4):
                last = nc.tensor.transpose(bank16[1][:, g * P:(g + 1) * P], g_mask[:, g * P:(g + 1) * P], id16[:, :])
            last.then_inc(S["route_t_m"], 1)

            def mm3(out, w, hi, lo, start=True, stop=True):
                mm(out, wh[:, w, :], hi, start=start, stop=False)
                mm(out, wh[:, w, :], lo, start=False, stop=False)
                return mm(out, wl[:, w, :], hi, start=False, stop=stop)

            def shared_block(c, i):
                mm3(bank[6][:, :], SW1 + i, nh[:, :], nl[:, :])
                mm3(bank[7][:, :], SW2 + i, nh[:, :], nl[:, :]).then_inc(S["ab_done"], 1)

            def stage_b(c, e):
                n = E * c + e
                here = has(c)
                if here and e == 0:
                    wait(pe, "nh_done", c + 1)
                    wait(pe, "nl_done", c + 1)
                    wait(pe, "zz_done", c)
                    wait(pe, "x2_done", c)
                    wait(pe, "mk_dma", 48 * (c + 1))
                    shared_block(c, 0)
                if here:
                    wait(pe, "xh_done", n + 1)
                    wait(pe, "xl_done", n + 1)
                    wait(pe, "silu_done", n - 1)
                    mm3(p1_bank[e % 2], W1 + e, xh[:, e % 4, :], xl[:, e % 4, :]).then_inc(S["p1_done"], 1)
                    wait(pe, "m3_done", n - 1)
                    mm3(p3_bank[e % 2], W3 + e, xh[:, e % 4, :], xl[:, e % 4, :], stop=False)
                    mm(p3_bank[e % 2], b3s[:, e, :], mk[:, bass.ds((c % 2) * CH, CH)], start=False, stop=True)\
                        .then_inc(S["p3_done"], 1)
                k = (e - 2) % E
                if step_exists(c, e, 2):
                    wait(pe, "silu_done", n - 1)
                    wait(pe, "prod_done", n - 3)
                    mm(p2_bank[k % 2], wf[:, W2 + k, :], hid_b[:, k % 4, :], start=True, stop=True).then_inc(S["p2_done"], 1)
                if here and e == 2:
                    wait(pe, "ga_done", 2 * c + 1)
                    wait(pe, "g_done", 2 * c + 1)
                    shared_block(c, 1)
                if here and e == 5:
                    wait(pe, "g_done", 2 * c + 2)
                    wait(pe, "ga_done", 2 * c + 2)
                    for i in range(2):
                        last = mm(bank[6][:, :], wf[:, SW3 + i, :], gg[:, i, :], start=i == 0, stop=i == 1)
                    last.then_inc(S["z_done"], 1)
                if e == 6 and has(c, 1):
                    wait(pe, "acc_done", E * c)
                    wait(pe, "g_done", 2 * c + 2 if here else 2 * NCH)
                    for t in range(TPC):
                        cols = slice(t * P, (t + 1) * P)
                        last = nc.tensor.transpose(bank[7][:, cols], yf[:, cols], id32[:, :])
                    last.then_inc(S["yt_done"], 1)

            pe.wait_ge(S["wh_done"], 1)
            pe.wait_ge(S["wl_done"], 1)
            pe.wait_ge(S["b3_ready"], 1)
            pe.wait_ge(S["trw_copied"], 1)
            steps(pe, stage_b)

            def stage_c(c):
                if has(c):
                    wait(pe, "n3_done", c + 1)
                    wait(pe, "n3t_done", c)
                    for t in range(TPC):
                        cols = slice(t * P, (t + 1) * P)
                        last = nc.tensor.transpose(bank[0][:, cols], n3[:, cols], id32[:, :])
                    last.then_inc(S["t3_done"], 1)
                    wait(pe, "vt_done", c)
                    mm(bank[1][:, :], wv[:, :], ctx_t[:, bass.ts(c, CH)], start=True, stop=True).then_inc(S["vt_pe"], 1)
                    wait(pe, "n3t_done", c + 1)
                    wait(pe, "qt_done", c)
                    mm(bank[2][:, :], wq[:, :], n3_t, start=True, stop=True).then_inc(S["qt_pe"], 1)
                if has(c, 1):
                    wait(pe, "exp_done", 2 * c)
                    wait(pe, "pt_done", c - 1)
                    for t in range(TPC):
                        last = nc.tensor.transpose(bank[4][:, t * P:(t + 1) * P], pr[:, t, :], id32[:, :])
                    last.then_inc(S["pt_pe"], 1)
                if has(c):
                    wait(pe, "qt_done", c + 1)
                    wait(pe, "vt_done", c + 1)
                    wait(pe, "sub_done", c)
                    for t in range(TPC):
                        for half in range(2):
                            cols = slice(t * P + half * SEQ, t * P + half * SEQ + SEQ)
                            last = mm(bank[5][half * SEQ:(half + 1) * SEQ, t * SEQ:(t + 1) * SEQ], q_t[:, cols],
                                      v_t[:, cols], start=True, stop=True)
                    last.then_inc(S["sc_pe"], 1)
                if has(c, 1):
                    wait(pe, "pt_done", c)
                    wait(pe, "v_done", c)
                    wait(pe, "x3_done", c - 1)
                    for t in range(TPC):
                        cols = slice(t * P, (t + 1) * P)
                        last = mm(bank[6][:, cols], pr_t[:, cols], v_tok[:, cols], start=True, stop=True)
                    last.then_inc(S["o3_pe"], 1)
                if has(c):
                    wait(pe, "v_done", c)
                    for t in range(TPC):
                        cols = slice(t * P, (t + 1) * P)
                        last = nc.tensor.transpose(bank[3][:, cols], v_t[:, cols], id32[:, :])
                    last.then_inc(S["v_pe"], 1)

            pe.wait_ge(S["c_weights"], 32)
            skewed(pe, stage_c, 2)

            def stage_d2(c):
                wait(pe, "magic_done", c + 1)
                wait(pe, "xq_done", c)
                for t in range(TPC):
                    cols = slice(t * P, (t + 1) * P)
                    last = nc.tensor.transpose(bank[0][:, cols], qn[:, cols], id32[:, :])
                last.then_inc(S["t4_done"], 1)
                wait(pe, "xq_done", c + 1)
                wait(pe, "h_done", 3 * c)
                for b in range(NB_FFN):
                    for k in (b, NB_FFN + b):
                        last = mm(bank[1 + k][:, :], wgq[:, k * P:(k + 1) * P], xq[:, :], start=True, stop=True)
                    last.then_inc(S["gu_done"], 1)

            stage_d2(0)
            with pe.Fori(1, NCH) as c:
                stage_d2(c)

            def stage_d3(c):
                wait(pe, "hq_done", c + 1)
                wait(pe, "scaled_done", c)
                for t in range(TPC):
                    for b in range(NB_FFN):
                        last = mm(bank[7][:, t * P:(t + 1) * P], hq[:, b * CH + t * P:b * CH + (t + 1) * P],
                                  wdq[:, b * P:(b + 1) * P], start=b == 0, stop=b == NB_FFN - 1)
                last.then_inc(S["down_done"], 1)

            stage_d3(0)
            with pe.Fori(1, NCH) as c:
                stage_d3(c)

        @block.scalar
        def _(act):
            A = nc.scalar.activation

            act.wait_ge(S["pool_consts"], 1)

            def stage_a(c):
                if has(c):
                    wait(act, "landed", c + 1)
                    wait(act, "s_done", c)
                    A(ctx_now, ctx_t[:, bass.ts(c, CH)], ACT.Copy).then_inc(S["ctx_copied"], 1)
                if has(c, 2):
                    wait(act, "stats2", c - 1)
                    A(sd[1][:, bass.ts(c - 2, TPC)], mv[1][:, bass.ts(c - 2, TPC), 1], ACT.Sqrt, bias=eps_t[:, :])\
                        .then_inc(S["sqrt2"], 1)
                if has(c):
                    wait(act, "stats1", c + 1)
                    A(sd[0][:, bass.ts(c, TPC)], mv[0][:, bass.ts(c, TPC), 1], ACT.Sqrt, bias=eps_t[:, :])\
                        .then_inc(S["sqrt1"], 1)
                if has(c, 3):
                    wait(act, "t2_done", c - 2)
                    wait(act, "logits_done", c - 3)
                    A(n2_now, bank[2][:, :], ACT.Copy).then_inc(S["n2_copied"], 1)
                    A(n2_t[:, bass.ts(c - 3, CH)], bank[2][:, :], ACT.Copy).then_inc(S["n2_stored"], 1)
                if has(c):
                    wait(act, "nb1_done", c + 1)
                    wait(act, "o_done", c)
                    wait(act, "base_done", c)
                    for t in range(TPC):
                        j = c * TPC + t
                        last = A(xn[:, t * P:(t + 1) * P], X[:, bass.ds(j * P, P)], ACT.Identity,
                                 scale=rs[0][:, bass.ds(j, 1)], bias=nb1[:, bass.ds(j, 1)])
                    last.then_inc(S["xn_done"], 1)

            for c in range(4):
                stage_a(c)
            act.wait_ge(S["wprep_pe"], 1)
            A(wgq[:, 0:512], bank16[4], ACT.Copy)
            A(wgq[:, 512:768], bank16[5][:, 0:256], ACT.Copy)
            A(wdq[:, :], bank16[6][:, 0:384], ACT.Copy)
            A(down_scale[:, :], bank[7][:, 0:P], ACT.Copy).then_inc(S["wprep_done"], 1)
            with act.Fori(4, NCH) as c:
                stage_a(c)
            act.wait_ge(S["weights_dma"], 32)
            A(wh[:, :, :], wstage, ACT.Copy).then_inc(S["wh_done"], 1)
            for c in range(NCH, NCH + 3):
                stage_a(c)

            act.wait_ge(S["shifted"], 1)
            A(g_sc, g_a, ACT.Exp).then_inc(S["exp_g"], 1)
            act.wait_ge(S["small_dma"], 112)
            A(sig[:, :], clip[:, :], ACT.Exp, scale=-1.0).then_inc(S["expclip"], 1)
            act.wait_ge(S["route_t_w"], 1)
            A(g_tr, bank[0][:, :], ACT.Copy).then_inc(S["trw_copied"], 1)
            act.wait_ge(S["route_t_m"], 1)
            A(g_mtr, bank16[1], ACT.Copy).then_inc(S["trm_copied"], 1)

            def stage_b(c, e):
                n = E * c + e
                here = has(c)
                if here and e in (3, 6):
                    i = e // 3 - 1
                    wait(act, "ab_done", 2 * c + i + 1)
                    wait(act, "g_done", 2 * c + i)
                    A(ga, bank[6][:, :], ACT.Silu).then_inc(S["ga_done"], 1)
                if e == 1 and has(c, 1):
                    wait(act, "z_done", c)
                    wait(act, "zz_added", c - 1)
                    A(zz, bank[6][:, :], ACT.Copy).then_inc(S["zz_done"], 1)
                k = (e - 3) % E
                if step_exists(c, e, 3):
                    wait(act, "p1_done", n - 2)
                    wait(act, "p2_done", n - 6)
                    A(hid_b[:, k % 4, :], p1_bank[k % 2], ACT.Silu, bias=bias[:, k:k + 1]).then_inc(S["silu_done"], 1)
                if here:
                    wait(act, "xs_done", n + 1)
                    wait(act, "p3_done", n - 3)
                    A(xh[:, e % 4, :], xs[:, e % 4, :], ACT.Copy).then_inc(S["xh_done"], 1)
                if step_exists(c, e, 3):
                    wait(act, "p3_done", n - 2)
                    wait(act, "prod_done", n - 6)
                    A(m3[:, k % 4, :], p3_bank[k % 2], ACT.Copy).then_inc(S["m3_done"], 1)
                if e == 6 and chunk_follows(c):
                    wait(act, "ab_done", 2 * (c + 1))
                    split_high(c + 1)

            def split_high(c):
                A(nh[:, :], n2_t[:, bass.ts(c, CH)], ACT.Copy).then_inc(S["nh_done"], 1)

            split_high(0)
            steps(act, stage_b)

            act.wait_ge(S["stats3"], NCH)
            A(sd[2][:, :], mv[2][:, :, 1], ACT.Sqrt, bias=eps_t[:, :]).then_inc(S["sqrt3"], 1)
            act.wait_ge(S["bqk_done"], 1)
            act.wait_ge(S["pr_zero"], 1)

            def stage_c(c):
                if has(c):
                    wait(act, "t3_done", c + 1)
                    wait(act, "qt_pe", c)
                    A(n3_t, bank[0][:, :], ACT.Copy).then_inc(S["n3t_done"], 1)
                    wait(act, "vt_pe", c + 1)
                    wait(act, "v_pe", c)
                    A(v_t, bank[1][:, :], ACT.Identity, bias=bias[:, 18:19]).then_inc(S["vt_done"], 1)
                    wait(act, "qt_pe", c + 1)
                    wait(act, "sc_pe", c)
                    A(q_t, bank[2][:, :], ACT.Identity, bias=bqk[:, :]).then_inc(S["qt_done"], 1)
                if has(c, 1):
                    wait(act, "pt_pe", c)
                    wait(act, "o3_pe", c - 1)
                    A(pr_t, bank[4][:, :], ACT.Copy).then_inc(S["pt_done"], 1)
                if has(c):
                    wait(act, "sub_done", c + 1)
                    wait(act, "pt_pe", c)
                    wait(act, "sum_done", c)
                    for half in range(2):
                        rows = slice(half * SEQ, (half + 1) * SEQ)
                        A(pr[rows, :, half * SEQ:(half + 1) * SEQ], sc[rows, :, :], ACT.Exp, scale=SCORE_SCALE)\
                            .then_inc(S["exp_done"], 1)
                    wait(act, "v_pe", c + 1)
                    wait(act, "o3_pe", c)
                    A(v_tok, bank[3][:, :], ACT.Copy).then_inc(S["v_done"], 1)

            skewed(act, stage_c, 2)

            act.wait_ge(S["stats4"], NCH)
            A(sd[3][:, :], mv[3][:, :, 1], ACT.Sqrt, bias=eps_t[:, :]).then_inc(S["sqrt4"], 1)
            act.wait_ge(S["nb4_done"], 1)
            with act.Fori(0, NCH) as c:
                for t in range(2):
                    j = c * TPC + t
                    last = A(arena[:, bass.ds(c * 3 * CH + t * P, P)], X[:, bass.ts(j, P)], ACT.Identity,
                             scale=rs[3][:, bass.ds(j, 1)], bias=nb4[:, bass.ds(j, 1)])
                last.then_inc(S["n4_act"], 1)
            act.wait_ge(S["qs_dve"], 1)

            def stage_d2(c):
                if has(c):
                    wait(act, "clamp_done", c + 1)
                    wait(act, "t4_done", c)
                    A(qn, arena[:, bass.ds(c * 3 * CH, CH)], ACT.Identity, scale=qs[:, 0, 3:4], bias=magic_t[:, :])\
                        .then_inc(S["magic_done"], 1)
                if has(c, 1):
                    for b in range(NB_FFN):
                        wait(act, "gu_done", 3 * (c - 1) + b + 1)
                        wait(act, "h_done", 3 * (c - 2) + b + 1)
                        A(sg[:, b * CH:(b + 1) * CH], bank[1 + b][:, :], ACT.Silu, scale=wgu_i[:, b:b + 1])\
                            .then_inc(S["sg_done"], 1)

            skewed(act, stage_d2, 2)
            act.wait_ge(S["qs_dve"], 2)
            with act.Fori(0, NCH) as c:
                wait(act, "hclamp_done", c + 1)
                hid = arena[:, bass.ds(c * 3 * CH, 3 * CH)]
                A(hid, hid, ACT.Identity, scale=qs[:, 1, 3:4], bias=magic_t[:, :]).then_inc(S["hmagic_done"], 1)

        @block.vector
        def _(dve):
            V = nc.vector

            dve.sem_inc(S["x2_done"], 1)
            dve.wait_ge(S["small_dma"], 112)
            V.tensor_reduce(wgu_s[:, 0:6], wgu_f, AX.X, ALU.max, apply_absolute_value=True)
            V.tensor_reduce(wgu_s[:, 6:7], wd_f, AX.X, ALU.max, apply_absolute_value=True).then_inc(S["amax_done"], 1)
            dve.wait_ge(S["amax_done"], 1)
            V.tensor_scalar(wgu_s[:, 0:7], wgu_s[:, 0:7], 1e-30, 1.0 / QMAX, ALU.max, ALU.mult).then_inc(S["amax_done"], 1)
            dve.wait_ge(S["amax_done"], 2)
            V.reciprocal(wgu_i[:, 0:7], wgu_s[:, 0:7]).then_inc(S["wscale_done"], 1)
            dve.wait_ge(S["wscale_done"], 1)
            for b in range(2 * NB_FFN):
                V.tensor_scalar(wgu_f[:, b, :], wgu_f[:, b, :], wgu_i[:, b:b + 1], MAGIC, ALU.mult, ALU.add)
            V.tensor_scalar(wd_f, wd_f, wgu_i[:, 6:7], MAGIC, ALU.mult, ALU.add).then_inc(S["wscale_done"], 1)
            dve.wait_ge(S["wscale_done"], 2)
            V.tensor_scalar(wgu_q, work[:, 0:768], MAGIC, None, ALU.subtract).then_inc(S["wgu_rounded"], 1)
            V.tensor_scalar(wd_q, wd_f, MAGIC, None, ALU.subtract).then_inc(S["wd_rounded"], 1)
            dve.wait_ge(S["consts"], 48)
            V.tensor_scalar(wd_diag, id32[:, :], wgu_s[:, 6:7], None, ALU.mult).then_inc(S["diag_done"], 1)
            V.tensor_tensor(bqk[:, :], bias[:, 16:17], bias[:, 17:18], ALU.add).then_inc(S["bqk_done"], 1)

            def stats_rows(norm, c):
                for t in range(TPC):
                    last = V.bn_stats(stat[:, norm % 2, t, :], X[:, bass.ds((c * TPC + t) * P, P)])
                last.then_inc(S[f"stat{norm + 1}_done"], 1)

            def stats_aggregate(norm, c):
                dve.wait_ge(S[f"stat{norm + 1}_done"], c + 1)
                dve.sem_inc(S["dve_held"], 1)
                for t in range(TPC):
                    last = V.bn_aggr(mv_now[:, norm % 2, t, :], stat[:, norm % 2, t, :])
                last.then_inc(S[f"aggr{norm + 1}_done"], 1)
                dve.wait_ge(S[f"aggr{norm + 1}_done"], c + 1)
                V.tensor_copy(mv[norm][:, bass.ds(c * TPC, TPC), :], mv_now[:, norm % 2, :, :]).then_inc(S[f"stats{norm + 1}"], 1)

            def stats(norm, c):
                stats_rows(norm, c)
                stats_aggregate(norm, c)

            def stage_a(c):
                if has(c, 2):
                    wait(dve, "o_done", c - 1)
                    wait(dve, "base_done", c - 1)
                    cols = bass.ts(c - 2, CH)
                    V.tensor_tensor(X[:, cols], X[:, cols], bank[1][:, :], ALU.add).then_inc(S["x1_done"], 1)
                    wait(dve, "x1_done", c - 1)
                    stats(1, c - 2)
                if has(c):
                    wait(dve, "landed", c + 1)
                    stats(0, c)
                if has(c, 2):
                    wait(dve, "sqrt2", c - 1)
                    V.reciprocal(rs[1][:, bass.ts(c - 2, TPC)], sd[1][:, bass.ts(c - 2, TPC)]).then_inc(S["recip2"], 1)
                if has(c):
                    wait(dve, "s_done", c + 1)
                    wait(dve, "o_done", c)
                    V.tensor_tensor(tile4(sm), tile4(bank[0][:, :]), cm[:, :].rearrange("p (a n) -> p a n", a=1)
                                    .broadcast_to([P, TPC, P]), ALU.mult).then_inc(S["sm_done"], 1)
                    wait(dve, "sqrt1", c + 1)
                    V.reciprocal(rs[0][:, bass.ts(c, TPC)], sd[0][:, bass.ts(c, TPC)]).then_inc(S["recip1"], 1)
                    wait(dve, "recip1", c + 1)
                    V.scalar_tensor_tensor(nb1[:, bass.ts(c, TPC)], mv[0][:, bass.ts(c, TPC), 0], -1.0,
                                           rs[0][:, bass.ts(c, TPC)], ALU.mult, ALU.mult).then_inc(S["nb1_done"], 1)

            skewed(dve, stage_a, 3)

            count = [0]

            def link(instruction):
                count[0] += 1
                instruction.then_inc(S["route"], 1)
                dve.wait_ge(S["route"], count[0])

            def by_expert(ap):
                return ap.rearrange("p (t e) -> p t e", e=E)

            def per_tile(ap):
                return ap.rearrange("p (t a) -> p t a", a=1).broadcast_to([P, NT, E])

            dve.wait_ge(S["logits_done"], NCH)
            dve.wait_ge(S["wprep_done"], 1)
            dve.wait_ge(S["b3_ready"], 1)
            link(V.tensor_reduce(g_m, logits, AX.X, ALU.max))
            V.tensor_tensor(by_expert(g_a), logits, per_tile(g_m), ALU.subtract).then_inc(S["shifted"], 1)
            dve.wait_ge(S["exp_g"], 1)
            link(V.tensor_reduce(g_r, by_expert(g_sc), AX.X, ALU.add))
            link(V.reciprocal(g_m, g_r))
            link(V.tensor_tensor(by_expert(g_sc), by_expert(g_sc), per_tile(g_m), ALU.mult))
            last_of = {}
            for src, hot in ((g_sc, g_b), (g_a, g_c)):
                link(V.tensor_reduce(g_m, by_expert(src), AX.X, ALU.max))
                link(V.tensor_tensor(by_expert(hot), by_expert(src), per_tile(g_m), ALU.is_equal))
                link(V.tensor_tensor(by_expert(hot), by_expert(hot), d8[:, :].rearrange("p (a e) -> p a e", a=1)
                                     .broadcast_to([P, NT, E]), ALU.mult))
                link(V.tensor_reduce(g_m, by_expert(hot), AX.X, ALU.max))
                link(V.tensor_tensor(by_expert(hot), by_expert(hot), per_tile(g_m), ALU.is_equal))
                if hot is g_b:
                    link(V.scalar_tensor_tensor(g_a, g_b, -2.0, g_sc, ALU.mult, ALU.add))
            link(V.tensor_tensor(g_b, g_b, g_c, ALU.add))
            V.tensor_tensor(g_a, g_sc, g_b, ALU.mult).then_inc(S["routed_w"], 1)
            V.tensor_copy(g_mask, g_b).then_inc(S["routed_m"], 1)
            dve.wait_ge(S["expclip"], 1)
            link(V.tensor_scalar(sig[:, :], sig[:, :], 1.0, None, ALU.add))
            link(V.reciprocal(sig[:, :], sig[:, :]))

            def stage_b(c, e):
                n = E * c + e
                here = has(c)
                if here:
                    half = e // 4
                    wait(dve, f"wb_dma{half}", 16 * (c + 1))
                    wait(dve, "xh_done", n - 3)
                    wait(dve, "xl_done", n - 3)
                    V.tensor_tensor(tile4(xs[:, e % 4, :]), tile4(n2_t[:, bass.ts(c, CH)]),
                                    wb[:, half, :, e % 4 * P:(e % 4 + 1) * P], ALU.mult).then_inc(S["xs_done"], 1)
                if step_exists(c, e, 1):
                    k = (e - 1) % E
                    wait(dve, "xh_done", n)
                    wait(dve, "p3_done", n - 4)
                    V.tensor_tensor(xl[:, k % 4, :], xs[:, k % 4, :], xh[:, k % 4, :].bitcast(fp32), ALU.subtract)\
                        .then_inc(S["xl_done"], 1)
                if step_exists(c, e, 5):
                    k = (e - 5) % E
                    wait(dve, "p2_done", n - 4)
                    wait(dve, "m3_done", n - 4)
                    wait(dve, "acc_done", n - 8)
                    V.scalar_tensor_tensor(prod[:, k % 4, :], p2_bank[k % 2], bias[:, 8 + k:9 + k], m3[:, k % 4, :],
                                           ALU.add, ALU.mult).then_inc(S["prod_done"], 1)
                if here and e in (3, 6):
                    i = e // 3 - 1
                    wait(dve, "ga_done", 2 * c + i + 1)
                    wait(dve, "z_done", c)
                    V.tensor_tensor(gg[:, i, :], bank[7][:, :], ga, ALU.mult).then_inc(S["g_done"], 1)
                if e == 7 and chunk_follows(c):
                    wait(dve, "ab_done", 2 * (c + 1))
                    split_low(c + 1)
                if e == 1 and has(c, 2):
                    wait(dve, "yt_done", c)
                    cols = bass.ts(c - 2, CH)
                    V.tensor_tensor(X[:, cols], X[:, cols], bank[7][:, :], ALU.add).then_inc(S["x2_done"], 1)
                if e == 2 and has(c, 2):
                    wait(dve, "x2_done", c)
                    stats_rows(2, c - 2)
                if e == 3 and has(c, 2):
                    stats_aggregate(2, c - 2)

            def split_low(c):
                wait(dve, "nh_done", c + 1)
                V.tensor_tensor(nl[:, :], n2_t[:, bass.ts(c, CH)], nh[:, :].bitcast(fp32), ALU.subtract)\
                    .then_inc(S["nl_done"], 1)

            split_low(0)
            steps(dve, stage_b)

            dve.wait_ge(S["sqrt3"], 1)
            V.reciprocal(rs[2][:, :], sd[2][:, :]).then_inc(S["recip3"], 1)

            def stage_c(c):
                if has(c):
                    wait(dve, "sc_pe", c + 1)
                    raw = bank[5][:, 0:TPC * SEQ].rearrange("p (t k) -> p t k", t=TPC)
                    V.tensor_reduce(mx[:, :], raw, AX.X, ALU.max).then_inc(S["max_done"], 1)
                    wait(dve, "max_done", c + 1)
                    wait(dve, "exp_done", 2 * c)
                    V.tensor_tensor(sc, raw, mx[:, :].rearrange("p (t a) -> p t a", a=1).broadcast_to([P, TPC, SEQ]),
                                    ALU.subtract).then_inc(S["sub_done"], 1)
                if has(c, 1):
                    wait(dve, "o3_pe", c)
                    wait(dve, "rinv_done", c)
                    for t in range(TPC):
                        x_tile = X[:, bass.ds((c - 1) * CH + t * P, P)]
                        last = V.scalar_tensor_tensor(x_tile, bank[6][:, t * P:(t + 1) * P], rinv[:, t:t + 1], x_tile,
                                                      ALU.mult, ALU.add)
                    last.then_inc(S["x3_done"], 1)
                    wait(dve, "x3_done", c)
                    stats(3, c - 1)
                if has(c):
                    wait(dve, "exp_done", 2 * (c + 1))
                    V.tensor_reduce(rsum[:, :], pr, AX.X, ALU.add).then_inc(S["sum_done"], 1)
                    wait(dve, "sum_done", c + 1)
                    V.reciprocal(rinv[:, :], rsum[:, :]).then_inc(S["rinv_done"], 1)

            skewed(dve, stage_c, 2)

            dve.wait_ge(S["sqrt4"], 1)
            V.reciprocal(rs[3][:, :], sd[3][:, :]).then_inc(S["recip4"], 1)
            dve.wait_ge(S["recip4"], 1)
            V.scalar_tensor_tensor(nb4[:, :], mv[3][:, :, 0], -1.0, rs[3][:, :], ALU.mult, ALU.mult).then_inc(S["nb4_done"], 1)
            dve.wait_ge(S["nb4_done"], 1)
            with dve.Fori(0, NCH) as c:
                for t in range(2, TPC):
                    j = c * TPC + t
                    last = V.tensor_scalar(arena[:, bass.ds(c * 3 * CH + t * P, P)], X[:, bass.ts(j, P)],
                                           rs[3][:, bass.ds(j, 1)], nb4[:, bass.ds(j, 1)], ALU.mult, ALU.add)
                last.then_inc(S["n4_dve"], 1)
                wait(dve, "n4_act", c + 1)
                wait(dve, "n4_dve", c + 1)
                V.tensor_reduce(am[:, 0, bass.ds(c, 1)], arena[:, bass.ds(c * 3 * CH, CH)], AX.X, ALU.max,
                                apply_absolute_value=True).then_inc(S["am_done"], 1)

            def quant_scale(j, last_max, value):
                first = j * 6
                dve.wait_ge(S[last_max], value)
                V.tensor_reduce(qs[:, j, 0:1], am[:, j, :], AX.X, ALU.max).then_inc(S["qs_step"], 1)
                dve.wait_ge(S["qs_all"], j + 1)
                V.scalar_tensor_tensor(qs[:, j, 2:3], qs[:, j, 1:2], 1.0 / QMAX, sig[:, j:j + 1], ALU.mult, ALU.mult)\
                    .then_inc(S["qs_step"], 1)
                dve.wait_ge(S["qs_step"], first + 2)
                V.reciprocal(qs[:, j, 3:4], qs[:, j, 2:3]).then_inc(S["qs_step"], 1)
                V.tensor_scalar(qs[:, j, 4:5], qs[:, j, 2:3], -QMAX - 1.0, None, ALU.mult).then_inc(S["qs_step"], 1)
                V.tensor_scalar(qs[:, j, 5:6], qs[:, j, 2:3], QMAX, None, ALU.mult).then_inc(S["qs_step"], 1)
                if j == 0:
                    V.tensor_scalar(wgu_i[:, 0:6], wgu_s[:, 0:6], qs[:, 0, 2:3], None, ALU.mult).then_inc(S["qs_step"], 1)
                else:
                    V.tensor_scalar(down_scale[:, :], down_scale[:, :], qs[:, 1, 2:3], None, ALU.mult)\
                        .then_inc(S["qs_step"], 1)
                dve.wait_ge(S["qs_step"], first + 6)
                dve.sem_inc(S["qs_dve"], 1)

            quant_scale(0, "am_done", NCH)

            def stage_d2(c):
                if has(c):
                    first = arena[:, bass.ds(c * 3 * CH, CH)]
                    V.tensor_scalar(first, first, qs[:, 0, 4:5], qs[:, 0, 5:6], ALU.max, ALU.min).then_inc(S["clamp_done"], 1)
                if has(c, 1):
                    for b in range(NB_FFN):
                        wait(dve, "sg_done", 3 * (c - 1) + b + 1)
                        V.scalar_tensor_tensor(arena[:, bass.ds((c - 1) * 3 * CH + b * CH, CH)], bank[4 + b][:, :],
                                               wgu_i[:, 3 + b:4 + b], sg[:, b * CH:(b + 1) * CH], ALU.mult, ALU.mult)\
                            .then_inc(S["h_done"], 1)
                if has(c):
                    wait(dve, "t4_done", c + 1)
                    wait(dve, "gu_done", 3 * c)
                    V.tensor_scalar(xq[:, :], bank[0][:, :], MAGIC, None, ALU.subtract).then_inc(S["xq_done"], 1)
                if has(c, 1):
                    wait(dve, "h_done", 3 * c)
                    V.tensor_reduce(am[:, 1, bass.ds(c - 1, 1)], arena[:, bass.ds((c - 1) * 3 * CH, 3 * CH)], AX.X, ALU.max,
                                    apply_absolute_value=True).then_inc(S["hmax_done"], 1)

            skewed(dve, stage_d2, 1)
            quant_scale(1, "hmax_done", NCH)

            def stage_d3(c):
                if has(c):
                    hid = arena[:, bass.ds(c * 3 * CH, 3 * CH)]
                    V.tensor_scalar(hid, hid, qs[:, 1, 4:5], qs[:, 1, 5:6], ALU.max, ALU.min).then_inc(S["hclamp_done"], 1)
                if has(c, 1):
                    wait(dve, "hmagic_done", c)
                    wait(dve, "down_done", c - 1)
                    V.tensor_scalar(hq, arena[:, bass.ds((c - 1) * 3 * CH, 3 * CH)], MAGIC, None, ALU.subtract)\
                        .then_inc(S["hq_done"], 1)
                if has(c, 2):
                    wait(dve, "down_done", c - 1)
                    wait(dve, "added_done", c - 2)
                    V.tensor_tensor(tile4(scaled[:, 0, :]), tile4(bank[7][:, :]),
                                    down_scale[:, :].rearrange("p (a n) -> p a n", a=1).broadcast_to([P, TPC, P]),
                                    ALU.mult).then_inc(S["scaled_done"], 1)

            skewed(dve, stage_d3, 3)

        @block.gpsimd
        def _(pool):
            G = nc.gpsimd

            G.memset(eps_t[:, :], EPS)
            G.memset(magic_t[:, :], MAGIC)
            G.memset(ones[:, :], 1.0)
            G.memset(mk[:, :], 0.0)
            G.memset(b3s[:, :, :], 0.0)
            pool.wait_ge(S["consts"], 48)
            G.tensor_copy(id16[:, :], id32[:, :]).then_inc(S["pool_consts"], 1)
            pool.wait_ge(S["pool_consts"], 1)

            count = [0]

            def link(instruction):
                count[0] += 1
                instruction.then_inc(S["b3_step"], 1)
                pool.wait_ge(S["b3_step"], count[0])

            pool.wait_ge(S["small_dma"], 112)
            link(G.tensor_copy(b3h[:, :], b3a))
            link(G.tensor_tensor(b3b, b3a, b3h[:, :], ALU.subtract))
            link(G.tensor_scalar(b3c, b3h[:, :], pick[:, 0:1], None, ALU.mult))
            for part in (1, 2):
                link(G.tensor_copy(b3h[:, :], b3b))
                link(G.tensor_tensor(b3b, b3b, b3h[:, :], ALU.subtract))
                link(G.tensor_scalar(b3a, b3h[:, :], pick[:, part:part + 1], None, ALU.mult))
                link(G.tensor_tensor(b3c, b3c, b3a, ALU.add))
            for e in range(E):
                last = G.tensor_scalar(b3s[0:24, e, :], b3c, pick[:, 3 + e:4 + e], None, ALU.mult)
            last.then_inc(S["b3_ready"], 1)

            def normalise(dst, norm, c, done):
                tiles = bass.ts(c, TPC)
                mean = mv[norm][:, tiles, 0:1].broadcast_to([P, TPC, P])
                inverse = rs[norm][:, tiles].rearrange("p (t a) -> p t a", a=1).broadcast_to([P, TPC, P])
                centred = f"centred{norm}"
                G.tensor_tensor(tile4(dst), tile4(X[:, bass.ts(c, CH)]), mean, ALU.subtract).then_inc(S[centred], 1)
                pool.wait_ge(S[centred], c + 1)
                G.tensor_tensor(tile4(dst), tile4(dst), inverse, ALU.mult).then_inc(S[done], 1)

            def stage_a(c):
                if has(c, 2):
                    wait(pool, "recip2", c - 1)
                    wait(pool, "t2_done", c - 2)
                    normalise(n2, 1, c - 2, "n2_done")
                if has(c):
                    wait(pool, "xn_done", c + 1)
                    cols = bass.ts(c, CH)
                    G.tensor_tensor(X[:, cols], X[:, cols], xn, ALU.add).then_inc(S["base_done"], 1)

            skewed(pool, stage_a, 3)
            pool.wait_ge(S["wh_done"], 1)
            G.tensor_tensor(wl[:, :, :], wstage, wh[:, :, :].bitcast(fp32), ALU.subtract).then_inc(S["wl_done"], 1)

            def stage_b(c):
                for e in range(1, E):
                    n = E * c + e
                    wait(pool, "prod_done", n + 1)
                    wait(pool, "acc_done", E * c if e == 1 else n)
                    if e == 5:
                        wait(pool, "zz_added", c + 1)
                    if e == 7:
                        wait(pool, "yt_done", c + 1)
                    G.tensor_tensor(yf if e == 7 else yy, prod[:, 0, :] if e == 1 else yy, prod[:, e % 4, :], ALU.add)\
                        .then_inc(S["acc_done"], 2 if e == 1 else 1)
                    if e == 4:
                        wait(pool, "acc_done", n + 1)
                        wait(pool, "zz_done", c + 1)
                        G.tensor_tensor(yy, yy, zz, ALU.add).then_inc(S["zz_added"], 1)

            stage_b(0)
            with pool.Fori(1, NCH) as c:
                stage_b(c)

            pool.wait_ge(S["x2_done"], NCH + 1)
            pool.wait_ge(S["xl_done"], E * NCH)
            pool.wait_ge(S["nh_done"], NCH)
            G.memset(pr, 0.0).then_inc(S["pr_zero"], 1)
            pool.wait_ge(S["recip3"], 1)

            def stage_c(c):
                wait(pool, "t3_done", c)
                normalise(n3, 2, c, "n3_done")

            stage_c(0)
            with pool.Fori(1, NCH) as c:
                stage_c(c)

            for j in range(2):
                pool.wait_ge(S["qs_step"], 6 * j + 1)
                G.partition_all_reduce(qs[:, j, 1:2], qs[:, j, 0:1], P, RMAX).then_inc(S["qs_all"], 1)
            with pool.Fori(0, NCH) as c:
                wait(pool, "scaled_done", c + 1)
                cols = bass.ts(c, CH)
                G.tensor_tensor(X[:, cols], X[:, cols], scaled[:, 0, :], ALU.add).then_inc(S["added_done"], 1)


def step_exists(c, e, lag):
    return not isinstance(c, int) or 0 <= E * c + e - lag < E * NCH


def chunk_follows(c):
    return not isinstance(c, int) or c < NCH - 1


def steps(engine, step):
    for n in range(E + E // 2):
        step(n // E, n % E)
    with engine.Fori(1, NCH - 1) as c:
        for e in range(E // 2, E):
            step(c, e)
        for e in range(E // 2):
            step(c + 1, e)
    for n in range(E * (NCH - 1) + E // 2, E * (NCH + 2)):
        step(n // E, n % E)


def kernel(x, ctx_1024, L0_ffn_gate_w, L0_ffn_w1, L0_ffn_b1, L0_ffn_w2, L0_ffn_b2, L0_ffn_w3, L0_ffn_b3, L0_ffn_sw1,
           L0_ffn_sw2, L0_ffn_sw3, L1_xattn_Wq, L1_xattn_bq, L1_xattn_qk_b, L1_xattn_Wv, L1_xattn_bv, L1_ffn_clip_x,
           L1_ffn_clip_down, L1_ffn_w_gate, L1_ffn_w_up, L1_ffn_w_down):
    import numpy as np
    import concourse.bacc as bacc
    from concourse.bass_utils import run_bass_kernel_spmd

    f32 = np.float32
    ctx2 = np.ascontiguousarray(np.asarray(ctx_1024).reshape(TOK, P).T)
    blocks = [L0_ffn_w1[e].T for e in range(E)] + [L0_ffn_w3[e].T for e in range(E)]
    blocks += [L0_ffn_sw1[i * P:(i + 1) * P].T for i in range(2)] + [L0_ffn_sw2[i * P:(i + 1) * P].T for i in range(2)]
    wall = np.concatenate([np.asarray(b) for b in blocks], axis=1)
    blocks = [L0_ffn_w2[e].T for e in range(E)] + [L0_ffn_sw3[:, i * P:(i + 1) * P].T for i in range(2)]
    wfull = np.concatenate([np.asarray(b) for b in blocks], axis=1)
    biases = np.concatenate([np.asarray(a) for a in (L0_ffn_b1.T, L0_ffn_b2.T, L1_xattn_bq[:, None],
                                                     L1_xattn_qk_b[:, None], L1_xattn_bv[:, None])], axis=1)
    wgu = np.zeros((P, 2 * NB_FFN, P), f32)
    for j, w in enumerate((L1_ffn_w_gate, L1_ffn_w_up)):
        for b in range(NB_FFN):
            rows = np.asarray(w[b * P:min((b + 1) * P, I_FFN)])
            wgu[:rows.shape[0], j * NB_FFN + b, :] = rows
    wd = np.zeros((P, NB_FFN * P), f32)
    wd[:, :I_FFN] = np.asarray(L1_ffn_w_down)
    ident = np.eye(P, dtype=f32)
    s, t = np.arange(P)[:, None], np.arange(P)[None, :]
    causal = ((s // SEQ == t // SEQ) & (s <= t)).astype(f32)
    down8 = np.tile(np.arange(E, 0, -1, dtype=f32), (P, 1))
    pick = np.zeros((3 * E, 3 + E), f32)
    for r in range(3 * E):
        pick[r, r // E] = 1.0
        pick[r, 3 + r % E] = 1.0
    ins = dict(
        x=np.asarray(x).reshape(TOK, P), ctxT=ctx2, wall=wall, wfull=wfull, biases=biases,
        b3rep=np.concatenate([np.asarray(L0_ffn_b3)] * 3, axis=0), b3pick=pick, gateT=np.asarray(L0_ffn_gate_w).T,
        wqT=np.asarray(L1_xattn_Wq).T, wvT=np.asarray(L1_xattn_Wv).T, wgu=wgu.reshape(P, -1), wd=wd,
        clips=np.concatenate([np.asarray(L1_ffn_clip_x), np.asarray(L1_ffn_clip_down)]), ident=ident, causal=causal,
        down8=down8)
    ins = {k: np.ascontiguousarray(v) for k, v in ins.items()}
    nc = bacc.Bacc("TRN2", target_bir_lowering=False, num_devices=1, dynamic_dma_scratch_size=1024)
    args = {k: nc.dram_tensor(f"in_{k}", v.shape, mybir.dt.from_np(v.dtype), kind="ExternalInput").ap() for k, v in ins.items()}
    args["out"] = nc.dram_tensor("out", (TOK, P), fp32, kind="ExternalOutput").ap()
    build(nc, **args)
    r = run_bass_kernel_spmd(nc, [{f"in_{k}": v for k, v in ins.items()}], core_ids=[0])
    return np.asarray(r.results[0]["out"]).reshape(P, SEQ, P)
```

```python
from contextlib import ExitStack

import concourse.bass as bass
from concourse import mybir

fp32 = mybir.dt.float32
fp32r = mybir.dt.float32r
bf16 = mybir.dt.bfloat16
i32 = mybir.dt.int32
ALU = mybir.AluOpType
ACT = mybir.ActivationFunctionType
AX = mybir.AxisListType
RMAX = bass.bass_isa.ReduceOp.max

P = 128
TOK = 8192
SEQ = 64
CH = 512
TPC = CH // P
NCH = TOK // CH
NT = TOK // P
EARLY = NT - 2 * TPC
E = 8
NB_FFN = 3
I_FFN = 352
EPS = 1e-5
QMAX = 127.0
MAGIC = 12582912.0
W1, W3, SW1, SW2, W2 = 0, 8, 16, 18, 20
NW = 28
SCORE_SCALE = (P / 16) ** -0.5


def build(nc, x, ctxT, wall, sw3T, biases, b3rep, b3pick, gateT, wqT, wvT, wgu, wd, clips, ident, causal, down8, out):
    x_v = x.rearrange("(t p) d -> p t d", p=P)
    out_v = out.rearrange("(t p) d -> p t d", p=P)
    weight_dram = nc.dram_tensor("weight_by_tile", (NT * E, P), fp32).ap()
    mask_dram = nc.dram_tensor("mask_by_tile", (NT * E, P), bf16).ap()

    with ExitStack() as ctx:
        def sb(name, shape, dt=fp32):
            return ctx.enter_context(nc.sbuf_tensor(name, shape, dt))

        def sem(name):
            return ctx.enter_context(nc.semaphore(name))

        def tile4(ap):
            return ap.rearrange("p (t n) -> p t n", t=TPC)

        X = sb("X", [P, TOK])
        arena = sb("arena", [P, 3 * TOK])
        ctx_t = arena[:, 0:TOK]
        n2_t = arena[:, TOK:2 * TOK]
        misc = arena[:, 2 * TOK:3 * TOK]
        ctx_now, sm, xn, n2, n2_now = (misc[:, i * 1024:(i + 1) * 1024].rearrange("p (b n) -> p b n", b=2) for i in range(5))
        wstage = misc[:, 5120:5120 + W2 * P].rearrange("p (b n) -> p b n", n=P)
        cm = misc[:, 7680:7808]
        wb = misc[:, 0:4096].rearrange("p (h t n) -> p h t n", h=2, t=TPC)
        m3 = misc[:, 4096:6144].rearrange("p (b n) -> p b n", b=4)
        prod = misc[:, 6144:8192].rearrange("p (b n) -> p b n", b=4)
        centred = misc
        n3, n3_t, q_t, v_t, v_tok, pr_t, pr_flat = (
            n2_t[:, i * 1024:(i + 1) * 1024].rearrange("p (b n) -> p b n", b=2) for i in range(7))
        pr = [tile4(pr_flat[:, p, :]) for p in range(2)]
        sc = n2_t[:, 7168:7680].rearrange("p (b t k) -> p b t k", b=2, t=TPC)

        wh = sb("wh", [P, NW, P], fp32r)
        wl = sb("wl", [P, NW, P], fp32r)
        nh = sb("nh", [P, CH], fp32r)
        nl = sb("nl", [P, CH], fp32r)
        xh = sb("xh", [P, 4, CH], fp32r)
        xl = sb("xl", [P, 4, CH], fp32r)
        w_sw3 = sb("w_sw3", [P, 2, P])
        xs = sb("xs", [P, 2, CH])
        hid_b = sb("hid_b", [P, 2, CH])
        hh = sb("hh", [P, 4, CH], fp32r)
        hl = sb("hl", [P, 2, CH], fp32r)
        w2stage = hid_b[:, :, :].rearrange("p b n -> p (b n)").rearrange("p (b n) -> p b n", n=P)
        gg = sb("gg", [P, 2, CH])
        work = sb("work", [P, 5 * CH])
        ga, zz, yy, yf = (work[:, i * CH:(i + 1) * CH] for i in range(4))
        b3a, b3b, b3c = (gg[0:24, 0, i * P:(i + 1) * P] for i in range(3))
        b3h = gg[0:24, 0, 3 * P:3 * P + P // 2].bitcast(bf16)
        wgu_all = gg[:, :, :].rearrange("p b n -> p (b n)")[:, 0:2 * NB_FFN * P]
        wgu_f = wgu_all.rearrange("p (b n) -> p b n", n=P)
        wd_f = work[:, 0:NB_FFN * P]
        wgu_q = xs[:, 0, 0:384].bitcast(bf16)
        wd_q = xs[:, 1, 0:192].bitcast(bf16)
        wd_diag = xs[:, 1, 192:320]
        ones = xs[:, 1, 320:448]
        wq = work[:, 2048:2176]
        wv = work[:, 2176:2304]
        HT = NT // 2
        GW = HT * E
        g_sc, g_b, g_c, g_tr, g_a = (work[:, first:first + GW] for first in (512, 768, 1536, 1792, 2048))
        g_mtr = work[:, 1536:1664].bitcast(bf16)
        g_mask = work[:, 2304:2432].bitcast(bf16)
        g_m = work[:, 2432:2464]
        g_r = work[:, 2464:2496]
        norm_q = xs
        norm_m = hid_b[:, 0, :]
        qn = hid_b[:, 1, :].bitcast(bf16).rearrange("p (b n) -> p b n", b=2)
        xq = gg[:, 0, :].bitcast(bf16).rearrange("p (b n) -> p b n", b=2)
        up_2 = gg[:, 1, :]
        sg = work[:, 0:NB_FFN * CH]
        hq = work[:, 0:NB_FFN * CH].bitcast(bf16).rearrange("p (b n) -> p b n", b=2)
        scaled = work[:, 1536:2560].rearrange("p (b n) -> p b n", b=2)

        mk = sb("mk", [P, 2 * CH], bf16)
        b3s = sb("b3s", [P, E, P], bf16)
        pick = sb("pick", [24, 3 + E])
        bias = sb("bias", [P, 19])
        bqk = sb("bqk", [P, 1])
        gate_w = sb("gate_w", [P, E])
        wgq = sb("wgq", [P, 2 * NB_FFN * P], bf16)
        wdq = sb("wdq", [P, NB_FFN * P], bf16)
        wgu_s = sb("wgu_s", [P, 8])
        wgu_i = sb("wgu_i", [P, 8])
        down_scale = sb("down_scale", [P, P])
        id32 = sb("id32", [P, P])
        id16 = sb("id16", [P, P], bf16)
        d8 = sb("d8", [P, E])
        eps_t = sb("eps_t", [P, 1])
        magic_t = sb("magic_t", [P, 1])
        clip = sb("clip", [P, 2])
        table_out = sb("table_out", [P, 1])
        sig = sb("sig", [P, 2])
        stat = sb("stat", [P, 2, TPC, 6])
        mv_now = sb("mv_now", [P, 2, TPC, 2])
        mv_a = sb("mv_a", [P, 2, 2, TPC, 2])
        sd_a = sb("sd_a", [P, 2, 2, TPC])
        rs_a = sb("rs_a", [P, 2, 2, TPC])
        nb_a = sb("nb_a", [P, 2, TPC])
        mv = [None, None] + [sb(f"mv{i}", [P, NT, 2]) for i in (2, 3)]
        sd = [None, None] + [sb(f"sd{i}", [P, NT]) for i in (2, 3)]
        rs = [None, None] + [sb(f"rs{i}", [P, NT]) for i in (2, 3)]
        mx = sb("mx", [P, TPC])
        rsum = sb("rsum", [P, TPC])
        rinv = sb("rinv", [P, 2, TPC])
        am = sb("am", [P, NCH])
        row_max = work[:, 1536:1536 + NT]
        norm_max = work[:, 1536 + NT:1536 + 2 * NT]
        step_scale = work[:, 1536 + 2 * NT:1536 + 3 * NT]
        minus_magic_t = sb("minus_magic_t", [P, 1])
        qs = sb("qs", [P, 2, 8])

        bank = [ctx.enter_context(nc.psum_tensor(f"bank{i}", [P, CH], fp32)) for i in range(8)]
        bank16 = [b[:, :].bitcast(bf16)[:, 0:CH] for b in bank]
        p1_bank = bank[2][:, :], bank[3][:, :]
        p2_bank = bank[1][:, :], bank[5][:, :]
        p3_bank = bank[0][:, :], bank[4][:, :]
        s_bank = bank[0][:, :], bank[4][:, :]
        o_bank = bank[1][:, :], bank[5][:, :]
        t2_bank = bank[2][:, :], bank[6][:, :]
        sc_bank = bank[5][:, 0:TPC * SEQ], bank[7][:, 0:TPC * SEQ]
        wgu_pe = bank[1][:, :].bitcast(bf16)[:, 0:2 * NB_FFN * P]
        wd_pe = bank[2][:, :].bitcast(bf16)[:, 0:NB_FFN * P]
        down_pe = bank[3][:, 0:P]
        t4_bank = bank16[0], bank16[7]
        down_bank = bank[0][:, :], bank[7][:, :]
        logits_bank = bank[3], bank[7]
        tr_bank = bank[0][:, 0:GW], bank[7][:, 0:GW]
        mtr_bank = bank16[4][:, 0:GW], bank[7][:, 384:512].bitcast(bf16)

        LOADS = [(0, 1), (1, 1), (2, 1), (3, 1), (4, 4), (8, 8)]
        x_dma = [sem(f"x_dma{i}") for i in range(len(LOADS))]
        c_dma = [sem(f"c_dma{i}") for i in range(len(LOADS))]
        names = """consts weights_dma small_dma landed tables pool_consts act_consts
            amax_done wscale_done wgu_rounded wd_rounded diag_done wprep_pe wprep_done bqk_done b3_step b3_ready
            stat1_done stats1 sqrt1 recip1 xn_done base_done ctx_copied s_done sm_done o_done x1_done stat2_done stats2
            sqrt2 recip2 n2_done t2_done n2_copied n2_stored logits_done wh_done wl_done
            route shifted exp_g expclip routed route_t tr_copied
            weight_stored mask_stored
            wb_dma0 wb_dma1 mk_dma nh_done nl_done xs_done xh_done xl_done p1_done p3_done p2_done
            silu_done hh_done hl_done zz_added m3_done prod_done acc_done ab_done ga_done g_done z_done
            zz_done yt_done x2_done stat3_done stats3 sqrt3 recip3 pr_zero
            n3_done t3_done n3t_done vt_pe vt_done qt_pe qt_done v_pe v_done sc_pe max_done sub_done exp_done
            sum_done rinv_done pt_pe pt_done probs_done o3_pe x3_done stat4_done stats4 sqrt4 recip4
            qs_step qs_own qs_dve qs_all step_done norm_q_done qn_done t4_done xq_done gu_done sg_done
            row_max_done centred4
            h_done hmax_done h2_done up_done norm_m_done hclamp_done hmagic_done hq_dve hq_act down_done scaled_done
            added_done out_dma c_weights d_weights
            sp_held dve_held aggr1_done aggr2_done aggr3_done aggr4_done nb1_done centred1 centred2""".split()
        S = {n: sem(n) for n in names}

        def has(c, lag=0):
            return not isinstance(c, int) or 0 <= c - lag < NCH

        def at(c, here):
            return isinstance(c, int) and c == here

        def paired(engine, slot, lag, head=8, peeled=0, first=0):
            for c in range(first, head):
                slot(c, c % 2)
            with engine.Fori(head // 2, (NCH - peeled) // 2) as j:
                slot(2 * j, 0)
                slot(2 * j + 1, 1)
            for c in range(NCH - peeled, NCH + lag):
                slot(c, c % 2)

        def wait(engine, name, value):
            if not isinstance(value, int) or value > 0:
                engine.wait_ge(S[name], value)

        block = ctx.enter_context(nc.Block())

        @block.sync
        def _(sp):
            def load(i):
                c0, n = LOADS[i]
                sp.dma_start(X[:, c0 * CH:(c0 + n) * CH].rearrange("p (t d) -> p t d", d=P),
                             x_v[:, c0 * TPC:(c0 + n) * TPC, :]).then_inc(x_dma[i], 16)
                if i >= 2:
                    sp.dma_start(ctx_t[:, c0 * CH:(c0 + n) * CH], ctxT[:, c0 * CH:(c0 + n) * CH]).then_inc(c_dma[i], 16)

            def arrived(i):
                sp.wait_ge(x_dma[i], 16)
                sp.wait_ge(c_dma[i], 16)
                sp.sem_inc(S["landed"], LOADS[i][1])

            load(0)
            load(1)
            for dst, src in ((id32, ident), (cm, causal), (gate_w, gateT)):
                sp.dma_start(dst[:, :], src).then_inc(S["consts"], 16)
            load(2)
            arrived(0)
            load(3)
            arrived(1)
            load(4)
            arrived(2)
            load(5)
            arrived(3)
            small = ((bias[:, :], biases), (d8[:, :], down8), (b3a, b3rep), (pick[:, :], b3pick),
                     (clip[:, :], clips.partition_broadcast(P)))
            for dst, src in small:
                sp.dma_start(dst, src).then_inc(S["small_dma"], 16)
            sp.dma_start(wstage, wall[:, 0:W2, :]).then_inc(S["weights_dma"], 16)
            sp.dma_start(w2stage, wall[:, W2:NW, :]).then_inc(S["weights_dma"], 16)
            sp.dma_start(w_sw3[:, :, :], sw3T).then_inc(S["weights_dma"], 16)
            for i in range(4, len(LOADS)):
                arrived(i)

            def store_routes(half):
                sp.wait_ge(S["tr_copied"], half + 1)
                rows = slice(half * GW, (half + 1) * GW)
                for dram, tr, stored in ((weight_dram, g_tr, "weight_stored"), (mask_dram, g_mtr, "mask_stored")):
                    sp.dma_start(dram[rows, :].rearrange("(g p) k -> p g k", p=P), tr.rearrange("p (g k) -> p g k", k=P))\
                        .then_inc(S[stored], 16)
                sp.wait_ge(S["weight_stored"], 16 * (half + 1))
                sp.wait_ge(S["mask_stored"], 16 * (half + 1))

            store_routes(0)

            w_v = weight_dram.rearrange("(c t e) k -> c t (e k)", t=TPC, e=E)
            k_v = mask_dram.rearrange("(c t e) k -> c e t k", t=TPC, e=E)

            def broadcast(c, half):
                src = w_v[bass.ds(c, 1), :, half * 512:half * 512 + 512]
                src = src.rearrange("c t n -> (c t) n").partition_broadcast(P)
                sp.dma_start(wb[:, half, :, :], src).then_inc(S[f"wb_dma{half}"], 16)

            def masks(c):
                for part in range(3):
                    dst = mk[part * E:(part + 1) * E, bass.ds((c % 2) * CH, CH)].rearrange("e (t k) -> e t k", t=TPC)
                    src = k_v[bass.ds(c, 1), :, :, :].rearrange("c e t k -> (c e) t k")
                    sp.dma_start(dst, src).then_inc(S["mk_dma"], 16)

            sp.wait_ge(S["pool_consts"], 1)
            masks(0)
            sp.wait_ge(S["o_done"], NCH)
            broadcast(0, 0)
            sp.wait_ge(S["base_done"], NCH)
            sp.wait_ge(S["t2_done"], NCH)
            broadcast(0, 1)
            sp.wait_ge(S["mk_dma"], 48)
            masks(1)

            def hold(name, value):
                sp.wait_ge(S[name], value)
                sp.sem_inc(S["sp_held"], 1)

            def next_chunk(c):
                hold("xs_done", E * c - 4)
                broadcast(c, 0)
                hold("xs_done", E * c)
                broadcast(c, 1)

            next_chunk(1)
            store_routes(1)
            sp.dma_start(wq, wqT).then_inc(S["c_weights"], 16)
            sp.dma_start(wv, wvT).then_inc(S["c_weights"], 16)
            with sp.Fori(2, NCH) as c:
                hold("mk_dma", 48 * c)
                hold("p3_done", E * (c - 1))
                masks(c)
                next_chunk(c)

            sp.wait_ge(S["z_done"], NCH)
            sp.dma_start(wgu_all, wgu).then_inc(S["d_weights"], 16)
            sp.dma_start(wd_f, wd).then_inc(S["d_weights"], 16)

            with sp.Fori(0, NCH) as c:
                hold("added_done", c + 1)
                sp.dma_start(out_v[:, bass.ts(c, TPC), :], X[:, bass.ts(c, CH)].rearrange("p (t d) -> p t d", d=P))\
                    .then_inc(S["out_dma"], 16)
            sp.wait_ge(S["out_dma"], 16 * NCH)

        @block.tensor
        def _(pe):
            mm = nc.tensor.matmul
            pe.sem_inc(S["yt_done"], 1)

            pe.wait_ge(S["consts"], 48)
            pe.wait_ge(S["pool_consts"], 1)

            def stage_a(c, p):
                if has(c):
                    wait(pe, "ctx_copied", c + 1)
                    wait(pe, "sm_done", c - 1)
                    for t in range(TPC):
                        tile = ctx_now[:, p, t * P:(t + 1) * P]
                        last = mm(s_bank[p][:, t * P:(t + 1) * P], tile, tile, start=True, stop=True)
                    last.then_inc(S["s_done"], 1)
                if has(c, 2):
                    wait(pe, "sm_done", c - 1)
                    wait(pe, "xn_done", c - 1)
                    wait(pe, "x1_done", c - 3)
                    for t in range(TPC):
                        cols = slice(t * P, (t + 1) * P)
                        last = mm(o_bank[p][:, cols], sm[:, p, cols], xn[:, p, cols], start=True, stop=True)
                    last.then_inc(S["o_done"], 1)
                if has(c, 5):
                    wait(pe, "n2_done", c - 4)
                    wait(pe, "n2_stored", c - 6)
                    for t in range(TPC):
                        cols = slice(t * P, (t + 1) * P)
                        last = nc.tensor.transpose(t2_bank[1 - p][:, cols], n2[:, 1 - p, cols], id32[:, :])
                    last.then_inc(S["t2_done"], 1)
                if has(c, 6):
                    wait(pe, "n2_copied", c - 5)
                    for t in range(TPC):
                        half = 1 if isinstance(c, int) and c - 6 >= NCH // 2 else 0
                        col = ((c - 6 - half * NCH // 2) * TPC + t) * E
                        last = mm(logits_bank[half][:, bass.ds(col, E)], n2_now[:, p, t * P:(t + 1) * P],
                                  gate_w[:, :], start=True, stop=True)
                    last.then_inc(S["logits_done"], 1)
                if at(c, 18):
                    transpose_routes(0)

            def transpose_routes(half):
                pe.wait_ge(S["routed"], half + 1)
                for g in range(2):
                    cols = slice(g * P, (g + 1) * P)
                    nc.tensor.transpose(tr_bank[half][:, cols], g_a[:, cols], id32[:, :])
                    last = nc.tensor.transpose(mtr_bank[half][:, cols], g_mask[:, cols], id16[:, :])
                last.then_inc(S["route_t"], 1)

            paired(pe, stage_a, 6, peeled=2)

            def mm3(out, w, hi, lo, start=True, stop=True):
                mm(out, wh[:, w, :], hi, start=start, stop=False)
                mm(out, wh[:, w, :], lo, start=False, stop=False)
                return mm(out, wl[:, w, :], hi, start=False, stop=stop)

            def shared_block(c, i):
                mm3(bank[6][:, :], SW1 + i, nh[:, :], nl[:, :])
                mm3(bank[7][:, :], SW2 + i, nh[:, :], nl[:, :]).then_inc(S["ab_done"], 1)

            def stage_b(c, e):
                n = E * c + e
                here = has(c)
                if here and e == 0:
                    wait(pe, "nh_done", c + 1)
                    wait(pe, "nl_done", c + 1)
                    wait(pe, "zz_done", c)
                    wait(pe, "x2_done", c)
                    wait(pe, "mk_dma", 48 * (c + 1))
                    if at(c, 1):
                        wait(pe, "tr_copied", 2)
                    shared_block(c, 0)
                if here:
                    wait(pe, "xh_done", n + 1)
                    wait(pe, "xl_done", n + 1)
                    wait(pe, "silu_done", n - 1)
                    wait(pe, "hh_done", n - 1)
                    mm3(p1_bank[e % 2], W1 + e, xh[:, e % 4, :], xl[:, e % 4, :]).then_inc(S["p1_done"], 1)
                    wait(pe, "m3_done", n - 1)
                    mm3(p3_bank[e % 2], W3 + e, xh[:, e % 4, :], xl[:, e % 4, :], stop=False)
                    if at(c, 0) and e == 0:
                        wait(pe, "b3_ready", 1)
                    mm(p3_bank[e % 2], b3s[:, e, :], mk[:, bass.ds((c % 2) * CH, CH)], start=False, stop=True)\
                        .then_inc(S["p3_done"], 1)
                k = (e - 3) % E
                if step_exists(c, e, 3):
                    wait(pe, "prod_done", n - 4)
                    wait(pe, "hh_done", n - 2)
                    wait(pe, "hl_done", n - 2)
                    mm3(p2_bank[k % 2], W2 + k, hh[:, k % 4, :], hl[:, k % 2, :]).then_inc(S["p2_done"], 1)
                if here and e == 2:
                    wait(pe, "ga_done", 2 * c + 1)
                    wait(pe, "g_done", 2 * c + 1)
                    shared_block(c, 1)
                if at(c, 0) and e == 6:
                    wait(pe, "g_done", 2)
                    transpose_routes(1)
                if here and e == 5:
                    wait(pe, "g_done", 2 * c + 2)
                    wait(pe, "ga_done", 2 * c + 2)
                    for i in range(2):
                        last = mm(bank[6][:, :], w_sw3[:, i, :], gg[:, i, :], start=i == 0, stop=i == 1)
                    last.then_inc(S["z_done"], 1)
                if at(c, NCH) and e == 4:
                    wait(pe, "c_weights", 32)
                    wait(pe, "m3_done", E * NCH)
                    wait(pe, "prod_done", E * NCH)
                    stage_c(0, 0)
                if e == 6 and has(c, 1):
                    wait(pe, "acc_done", E * c)
                    wait(pe, "g_done", 2 * c + 2 if here else 2 * NCH)
                    for t in range(TPC):
                        cols = slice(t * P, (t + 1) * P)
                        last = nc.tensor.transpose(bank[7][:, cols], yf[:, cols], id32[:, :])
                    last.then_inc(S["yt_done"], 1)

            pe.wait_ge(S["wh_done"], 1)
            pe.wait_ge(S["wl_done"], 2)
            pe.wait_ge(S["n2_stored"], NCH)
            pe.wait_ge(S["shifted"], 2)
            pe.wait_ge(S["tr_copied"], 1)

            def stage_c(c, p):
                if has(c):
                    wait(pe, "n3_done", c + 1)
                    wait(pe, "n3t_done", c)
                    for t in range(TPC):
                        cols = slice(t * P, (t + 1) * P)
                        last = nc.tensor.transpose(bank[0][:, cols], n3[:, p, cols], id32[:, :])
                    last.then_inc(S["t3_done"], 1)
                    wait(pe, "vt_done", c)
                    mm(bank[1][:, :], wv[:, :], ctx_t[:, bass.ts(c, CH)], start=True, stop=True).then_inc(S["vt_pe"], 1)
                if has(c, 2):
                    wait(pe, "probs_done", c - 1)
                    wait(pe, "pt_done", c - 2)
                    for t in range(TPC):
                        last = nc.tensor.transpose(bank[4][:, t * P:(t + 1) * P], pr[p][:, t, :], id32[:, :])
                    last.then_inc(S["pt_pe"], 1)
                if has(c):
                    wait(pe, "n3t_done", c + 1)
                    wait(pe, "qt_done", c)
                    mm(bank[2][:, :], wq[:, :], n3_t[:, p, :], start=True, stop=True).then_inc(S["qt_pe"], 1)
                if has(c, 1):
                    wait(pe, "vt_done", c)
                    wait(pe, "v_done", c - 1)
                    for t in range(TPC):
                        cols = slice(t * P, (t + 1) * P)
                        last = nc.tensor.transpose(bank[3][:, cols], v_t[:, 1 - p, cols], id32[:, :])
                    last.then_inc(S["v_pe"], 1)
                if has(c, 2):
                    wait(pe, "pt_done", c - 1)
                    wait(pe, "v_done", c - 1)
                    wait(pe, "x3_done", c - 2)
                    for t in range(TPC):
                        cols = slice(t * P, (t + 1) * P)
                        last = mm(bank[6][:, cols], pr_t[:, p, cols], v_tok[:, p, cols], start=True, stop=True)
                    last.then_inc(S["o3_pe"], 1)
                if has(c):
                    wait(pe, "qt_done", c + 1)
                    wait(pe, "vt_done", c + 1)
                    wait(pe, "sub_done", c - 1)
                    if at(c, 1):
                        wait(pe, "x2_done", NCH + 1)
                    for t in range(TPC):
                        for half in range(2):
                            cols = slice(t * P + half * SEQ, t * P + half * SEQ + SEQ)
                            last = mm(sc_bank[p][half * SEQ:(half + 1) * SEQ, t * SEQ:(t + 1) * SEQ], q_t[:, p, cols],
                                      v_t[:, p, cols], start=True, stop=True)
                    last.then_inc(S["sc_pe"], 1)

            steps(pe, stage_b)
            paired(pe, stage_c, 2, head=4, first=1)

            pe.wait_ge(S["vt_done"], NCH)
            pe.wait_ge(S["qt_done"], NCH)
            pe.wait_ge(S["v_done"], NCH)
            pe.wait_ge(S["pr_zero"], 1)
            pe.wait_ge(S["wgu_rounded"], 1)
            for b in range(2 * NB_FFN):
                nc.tensor.transpose(wgu_pe[:, b * P:(b + 1) * P], wgu_q[:, b * P:(b + 1) * P], id16[:, :])
            pe.wait_ge(S["wd_rounded"], 1)
            for b in range(NB_FFN):
                nc.tensor.transpose(wd_pe[:, b * P:(b + 1) * P], wd_q[:, b * P:(b + 1) * P], id16[:, :])
            pe.wait_ge(S["diag_done"], 1)
            mm(down_pe, ones[:, :], wd_diag, start=True, stop=True).then_inc(S["wprep_pe"], 1)

            def gate_and_up(c, p, i, b):
                if not has(c, 2):
                    return
                wait(pe, "xq_done", c - 1)
                if b == 2:
                    wait(pe, "up_done", c - 2)
                else:
                    wait(pe, "h_done", 2 * (c - 3) + i)
                for k in (b, NB_FFN + b):
                    last = mm(bank[1 + k][:, :], wgq[:, k * P:(k + 1) * P], xq[:, p, :], start=True, stop=True)
                last.then_inc(S["gu_done"], 1)

            def stage_d1(c, p):
                gate_and_up(c, p, 0, 2)
                if has(c, 1):
                    wait(pe, "qn_done", c)
                    wait(pe, "xq_done", c - 2)
                    for t in range(TPC):
                        cols = slice(t * P, (t + 1) * P)
                        last = nc.tensor.transpose(t4_bank[1 - p][:, cols], qn[:, 1 - p, cols], id16[:, :])
                    last.then_inc(S["t4_done"], 1)
                gate_and_up(c, p, 1, 0)
                gate_and_up(c, p, 2, 1)

            pe.wait_ge(S["wprep_done"], 1)
            paired(pe, stage_d1, 2, head=4)

            def stage_d2(c, p):
                wait(pe, "hq_dve", c + 1)
                wait(pe, "hq_act", c + 1)
                wait(pe, "scaled_done", c - 1)
                for t in range(TPC):
                    for b in range(NB_FFN):
                        last = mm(down_bank[p][:, t * P:(t + 1) * P], hq[:, p, b * CH + t * P:b * CH + (t + 1) * P],
                                  wdq[:, b * P:(b + 1) * P], start=b == 0, stop=b == NB_FFN - 1)
                last.then_inc(S["down_done"], 1)

            paired(pe, stage_d2, 0, head=2)

        @block.scalar
        def _(act):
            A = nc.scalar.activation

            for i in range(2):
                cols = slice(LOADS[i][0] * CH, (LOADS[i][0] + LOADS[i][1]) * CH)
                act.dma_start(ctx_t[:, cols], ctxT[:, cols]).then_inc(c_dma[i], 16)
            act.wait_ge(S["act_consts"], 1)

            def load_table(function):
                A(table_out[:, :], eps_t[:, :], function).then_inc(S["tables"], 1)

            load_table(ACT.Sqrt)

            def stage_a(c, p):
                if has(c, 1):
                    wait(act, "aggr1_done", c)
                    wait(act, "recip1", c - 2)
                    A(sd_a[:, 0, 1 - p, :], mv_a[:, 0, 1 - p, :, 1], ACT.Sqrt, bias=eps_t[:, :]).then_inc(S["sqrt1"], 1)
                if has(c):
                    wait(act, "landed", c + 1)
                    wait(act, "s_done", c - 1)
                    A(ctx_now[:, p, :], ctx_t[:, bass.ts(c, CH)], ACT.Copy).then_inc(S["ctx_copied"], 1)
                if has(c, 4):
                    wait(act, "aggr2_done", c - 3)
                    wait(act, "recip2", c - 5)
                    A(sd_a[:, 1, p, :], mv_a[:, 1, p, :, 1], ACT.Sqrt, bias=eps_t[:, :]).then_inc(S["sqrt2"], 1)
                if has(c, 6):
                    wait(act, "t2_done", c - 5)
                    wait(act, "logits_done", c - 7)
                    A(n2_now[:, p, :], t2_bank[p], ACT.Copy).then_inc(S["n2_copied"], 1)
                    A(n2_t[:, bass.ts(c - 6, CH)], t2_bank[p], ACT.Copy).then_inc(S["n2_stored"], 1)
                if has(c, 1):
                    wait(act, "nb1_done", c)
                    wait(act, "o_done", c - 2)
                    wait(act, "base_done", c - 2)
                    for t in range(TPC):
                        last = A(xn[:, 1 - p, t * P:(t + 1) * P], X[:, bass.ds(((c - 1) * TPC + t) * P, P)], ACT.Identity,
                                 scale=rs_a[:, 0, 1 - p, t:t + 1], bias=nb_a[:, 1 - p, t:t + 1])
                    last.then_inc(S["xn_done"], 1)
                if at(c, 14):
                    route_exp(0)
                if isinstance(c, int) and c in (16, 17):
                    act.wait_ge(S["weights_dma"], 48)
                    if c == 16:
                        A(wh[:, W2:NW, :], w2stage, ACT.Copy)
                    else:
                        A(wh[:, 0:W2, :], wstage, ACT.Copy).then_inc(S["wh_done"], 1)
                if at(c, 18):
                    copy_routes(0)
                    split_high(0)

            def split_high(c):
                A(nh[:, :], n2_t[:, bass.ts(c, CH)], ACT.Copy).then_inc(S["nh_done"], 1)

            def route_exp(half):
                act.wait_ge(S["shifted"], half + 1)
                A(g_sc, g_a, ACT.Exp).then_inc(S["exp_g"], 1)

            def copy_routes(half):
                act.wait_ge(S["route_t"], half + 1)
                A(g_tr, tr_bank[half], ACT.Copy)
                A(g_mtr, mtr_bank[half], ACT.Copy).then_inc(S["tr_copied"], 1)

            paired(act, stage_a, 6, peeled=2)
            route_exp(1)
            act.wait_ge(S["small_dma"], 80)
            A(sig[:, :], clip[:, :], ACT.Exp, scale=-1.0).then_inc(S["expclip"], 1)
            load_table(ACT.Silu)

            def stage_b(c, e):
                n = E * c + e
                here = has(c)
                if at(c, 1) and e == 1:
                    copy_routes(1)
                if here and e in (3, 6):
                    i = e // 3 - 1
                    wait(act, "ab_done", 2 * c + i + 1)
                    wait(act, "g_done", 2 * c + i)
                    A(ga, bank[6][:, :], ACT.Silu).then_inc(S["ga_done"], 1)
                if e == 1 and has(c, 1):
                    wait(act, "z_done", c)
                    wait(act, "zz_added", c - 1)
                    A(zz, bank[6][:, :], ACT.Copy).then_inc(S["zz_done"], 1)
                k = (e - 3) % E
                if step_exists(c, e, 3):
                    wait(act, "p1_done", n - 2)
                    wait(act, "hl_done", n - 4)
                    A(hid_b[:, k % 2, :], p1_bank[k % 2], ACT.Silu, bias=bias[:, k:k + 1]).then_inc(S["silu_done"], 1)
                    wait(act, "p2_done", n - 6)
                    A(hh[:, k % 4, :], p1_bank[k % 2], ACT.Silu, bias=bias[:, k:k + 1]).then_inc(S["hh_done"], 1)
                if here:
                    wait(act, "xs_done", n + 1)
                    wait(act, "p3_done", n - 3)
                    A(xh[:, e % 4, :], xs[:, e % 2, :], ACT.Copy).then_inc(S["xh_done"], 1)
                if step_exists(c, e, 3):
                    wait(act, "p3_done", n - 2)
                    wait(act, "prod_done", n - 6)
                    A(m3[:, k % 4, :], p3_bank[k % 2], ACT.Copy).then_inc(S["m3_done"], 1)
                if at(c, NCH) and e == 3:
                    sqrt3(0)
                if e == 6 and chunk_follows(c):
                    wait(act, "ab_done", 2 * (c + 1))
                    split_high(c + 1)

            def sqrt3(part):
                tiles = slice(0, EARLY) if part == 0 else slice(EARLY, NT)
                act.wait_ge(S["stats3"], NCH if part else NCH - 2)
                A(sd[2][:, tiles], mv[2][:, tiles, 1], ACT.Sqrt, bias=eps_t[:, :]).then_inc(S["sqrt3"], 1)

            steps(act, stage_b)

            act.wait_ge(S["bqk_done"], 1)
            act.wait_ge(S["pr_zero"], 1)

            def stage_c(c, p):
                if has(c):
                    wait(act, "t3_done", c + 1)
                    wait(act, "qt_pe", c - 1)
                    A(n3_t[:, p, :], bank[0][:, :], ACT.Copy).then_inc(S["n3t_done"], 1)
                    wait(act, "vt_pe", c + 1)
                    wait(act, "v_pe", c - 1)
                    wait(act, "sc_pe", c - 1)
                    A(v_t[:, p, :], bank[1][:, :], ACT.Identity, bias=bias[:, 18:19]).then_inc(S["vt_done"], 1)
                if has(c, 2):
                    wait(act, "pt_pe", c - 1)
                    wait(act, "o3_pe", c - 3)
                    A(pr_t[:, p, :], bank[4][:, :], ACT.Copy).then_inc(S["pt_done"], 1)
                if at(c, 1):
                    sqrt3(1)
                if has(c, 1):
                    wait(act, "sub_done", c)
                    wait(act, "pt_pe", c - 2)
                    for half in range(2):
                        rows = slice(half * SEQ, (half + 1) * SEQ)
                        A(pr[1 - p][rows, :, half * SEQ:(half + 1) * SEQ], sc[rows, 1 - p, :, :], ACT.Exp, scale=SCORE_SCALE)\
                            .then_inc(S["exp_done"], 1)
                if has(c):
                    wait(act, "qt_pe", c + 1)
                    A(q_t[:, p, :], bank[2][:, :], ACT.Identity, bias=bqk[:, :]).then_inc(S["qt_done"], 1)
                if has(c, 1):
                    wait(act, "v_pe", c)
                    wait(act, "o3_pe", c - 2)
                    A(v_tok[:, 1 - p, :], bank[3][:, :], ACT.Copy).then_inc(S["v_done"], 1)

            paired(act, stage_c, 2, head=4)

            for tiles, chunks in ((slice(0, EARLY), NCH - 2), (slice(EARLY, NT), NCH)):
                act.wait_ge(S["stats4"], chunks)
                A(sd[3][:, tiles], mv[3][:, tiles, 1], ACT.Sqrt, bias=eps_t[:, :]).then_inc(S["sqrt4"], 1)
            load_table(ACT.Silu)
            act.wait_ge(S["wprep_pe"], 1)
            A(wgq[:, :], wgu_pe, ACT.Copy)
            A(wdq[:, :], wd_pe, ACT.Copy)
            A(down_scale[:, :], down_pe, ACT.Copy).then_inc(S["wprep_done"], 1)
            act.wait_ge(S["step_done"], 1)

            def gate(c, p, i, b):
                wait(act, "gu_done", 3 * (c - 2) + i + 1)
                if b == 2:
                    wait(act, "h2_done", c - 2)
                else:
                    wait(act, "h_done", 2 * (c - 3) + i)
                A(sg[:, b * CH:(b + 1) * CH], bank[1 + b][:, :], ACT.Silu, scale=wgu_i[:, b:b + 1])\
                    .then_inc(S["sg_done"], 1)

            def stage_d1(c, p):
                if has(c, 2):
                    gate(c, p, 0, 2)
                    A(up_2, bank[6][:, :], ACT.Identity, scale=wgu_i[:, 5:6]).then_inc(S["up_done"], 1)
                if has(c, 1):
                    wait(act, "t4_done", c)
                    wait(act, "gu_done", 3 * (c - 2))
                    A(xq[:, 1 - p, :], t4_bank[1 - p], ACT.Copy).then_inc(S["xq_done"], 1)
                if has(c, 2):
                    gate(c, p, 1, 0)
                    gate(c, p, 2, 1)

            paired(act, stage_d1, 2, head=4)
            act.wait_ge(S["qs_dve"], 2)

            def stage_d2(c, p):
                if has(c, 2):
                    wait(act, "hmagic_done", c - 1)
                    wait(act, "down_done", c - 3)
                    A(hq[:, p, 2 * CH:3 * CH], arena[:, bass.ds(((c - 2) * 3 + 2) * CH, CH)], ACT.Identity,
                      bias=minus_magic_t[:, :]).then_inc(S["hq_act"], 1)
                if has(c):
                    wait(act, "hclamp_done", c + 1)
                    hid = arena[:, bass.ds(c * 3 * CH, 3 * CH)]
                    A(hid, hid, ACT.Identity, scale=qs[:, 1, 3:4], bias=magic_t[:, :]).then_inc(S["hmagic_done"], 1)

            paired(act, stage_d2, 2, head=4)

        @block.vector
        def _(dve):
            V = nc.vector

            dve.sem_inc(S["x2_done"], 1)
            def prepare_d():
                dve.wait_ge(S["d_weights"], 32)
                V.tensor_reduce(wgu_s[:, 0:6], wgu_f, AX.X, ALU.max, apply_absolute_value=True)
                V.tensor_reduce(wgu_s[:, 6:7], wd_f, AX.X, ALU.max, apply_absolute_value=True).then_inc(S["amax_done"], 1)
                dve.wait_ge(S["amax_done"], 1)
                V.tensor_scalar(wgu_s[:, 0:7], wgu_s[:, 0:7], 1e-30, 1.0 / QMAX, ALU.max, ALU.mult).then_inc(S["amax_done"], 1)
                dve.wait_ge(S["amax_done"], 2)
                V.reciprocal(wgu_i[:, 0:7], wgu_s[:, 0:7]).then_inc(S["wscale_done"], 1)
                dve.wait_ge(S["wscale_done"], 1)
                for b in range(2 * NB_FFN):
                    V.tensor_scalar(wgu_f[:, b, :], wgu_f[:, b, :], wgu_i[:, b:b + 1], MAGIC, ALU.mult, ALU.add)
                V.tensor_scalar(wd_f, wd_f, wgu_i[:, 6:7], MAGIC, ALU.mult, ALU.add).then_inc(S["wscale_done"], 1)
                dve.wait_ge(S["wscale_done"], 2)
                V.tensor_scalar(wgu_q, wgu_all, MAGIC, None, ALU.subtract).then_inc(S["wgu_rounded"], 1)
                V.tensor_scalar(wd_q, wd_f, MAGIC, None, ALU.subtract).then_inc(S["wd_rounded"], 1)
                V.tensor_scalar(wd_diag, id32[:, :], wgu_s[:, 6:7], None, ALU.mult).then_inc(S["diag_done"], 1)

            def stats_rows(norm, c):
                for t in range(TPC):
                    last = V.bn_stats(stat[:, norm % 2, t, :], X[:, bass.ds((c * TPC + t) * P, P)])
                last.then_inc(S[f"stat{norm + 1}_done"], 1)

            def stats_aggregate(norm, c):
                dve.wait_ge(S[f"stat{norm + 1}_done"], c + 1)
                dve.sem_inc(S["dve_held"], 1)
                for t in range(TPC):
                    last = V.bn_aggr(mv_now[:, norm % 2, t, :], stat[:, norm % 2, t, :])
                last.then_inc(S[f"aggr{norm + 1}_done"], 1)

            def stats_keep(norm, c):
                dve.wait_ge(S[f"aggr{norm + 1}_done"], c + 1)
                V.tensor_copy(mv[norm][:, bass.ds(c * TPC, TPC), :], mv_now[:, norm % 2, :, :]).then_inc(S[f"stats{norm + 1}"], 1)

            def rows_a(norm, c):
                wait(dve, f"aggr{norm + 1}_done", c)
                stats_rows(norm, c)

            def aggregate_a(norm, c, p, used):
                for name in used:
                    wait(dve, name, c - 1)
                wait(dve, f"stat{norm + 1}_done", c + 1)
                dve.sem_inc(S["dve_held"], 1)
                for t in range(TPC):
                    last = V.bn_aggr(mv_a[:, norm, p, t, :], stat[:, norm, t, :])
                last.then_inc(S[f"aggr{norm + 1}_done"], 1)

            def stage_a(c, p):
                if has(c):
                    wait(dve, "landed", c + 1)
                    rows_a(0, c)
                if has(c, 1):
                    wait(dve, "sqrt1", c)
                    wait(dve, "xn_done", c - 2)
                    V.reciprocal(rs_a[:, 0, 1 - p, :], sd_a[:, 0, 1 - p, :]).then_inc(S["recip1"], 1)
                if has(c, 4):
                    aggregate_a(1, c - 4, p, ("sqrt2", "centred1"))
                if has(c, 1):
                    wait(dve, "recip1", c)
                    V.scalar_tensor_tensor(nb_a[:, 1 - p, :], mv_a[:, 0, 1 - p, :, 0], -1.0, rs_a[:, 0, 1 - p, :],
                                           ALU.mult, ALU.mult).then_inc(S["nb1_done"], 1)
                if has(c, 3):
                    wait(dve, "o_done", c - 2)
                    wait(dve, "base_done", c - 2)
                    cols = bass.ts(c - 3, CH)
                    V.tensor_tensor(X[:, cols], X[:, cols], o_bank[1 - p], ALU.add).then_inc(S["x1_done"], 1)
                if has(c):
                    aggregate_a(0, c, p, ("sqrt1", "nb1_done"))
                if has(c, 1):
                    wait(dve, "s_done", c)
                    wait(dve, "o_done", c - 2)
                    V.tensor_tensor(tile4(sm[:, 1 - p, :]), tile4(s_bank[1 - p]), cm[:, :].rearrange("p (a n) -> p a n", a=1)
                                    .broadcast_to([P, TPC, P]), ALU.mult).then_inc(S["sm_done"], 1)
                if isinstance(c, int) and c in (15, 16, 17):
                    route(0, 2 * c - 29)
                if has(c, 4):
                    wait(dve, "sqrt2", c - 3)
                    wait(dve, "n2_done", c - 5)
                    V.reciprocal(rs_a[:, 1, p, :], sd_a[:, 1, p, :]).then_inc(S["recip2"], 1)
                if has(c, 3):
                    wait(dve, "x1_done", c - 2)
                    rows_a(1, c - 3)
                if isinstance(c, int) and c in (14, 15, 16, 17):
                    route(0, 2 * c - 28)

            count = [0]

            def link(instruction):
                count[0] += 1
                instruction.then_inc(S["route"], 1)
                dve.wait_ge(S["route"], count[0])

            def by_expert(ap):
                return ap.rearrange("p (t e) -> p t e", e=E)

            def per_tile(ap):
                return ap.rearrange("p (t a) -> p t a", a=1).broadcast_to([P, HT, E])

            def route(half, part):
                first = d8[:, :].rearrange("p (a e) -> p a e", a=1).broadcast_to([P, HT, E])
                if part == 0:
                    dve.wait_ge(S["logits_done"], (half + 1) * NCH // 2)
                    dve.wait_ge(S["small_dma"], 80)
                    logits = by_expert(logits_bank[half][:, 0:GW])
                    link(V.tensor_reduce(g_m, logits, AX.X, ALU.max))
                    if half == 1:
                        dve.wait_ge(S["route_t"], 1)
                    V.tensor_tensor(by_expert(g_a), logits, per_tile(g_m), ALU.subtract).then_inc(S["shifted"], 1)
                if part == 1:
                    dve.wait_ge(S["exp_g"], half + 1)
                    link(V.tensor_reduce(g_r, by_expert(g_sc), AX.X, ALU.add))
                    link(V.reciprocal(g_m, g_r))
                    link(V.tensor_tensor(by_expert(g_sc), by_expert(g_sc), per_tile(g_m), ALU.mult))
                if part in (2, 4):
                    src, hot = (g_sc, g_b) if part == 2 else (g_a, g_c)
                    link(V.tensor_reduce(g_m, by_expert(src), AX.X, ALU.max))
                    link(V.tensor_tensor(by_expert(hot), by_expert(src), per_tile(g_m), ALU.is_equal))
                    link(V.tensor_tensor(by_expert(hot), by_expert(hot), first, ALU.mult))
                if part in (3, 5):
                    hot = g_b if part == 3 else g_c
                    link(V.tensor_reduce(g_m, by_expert(hot), AX.X, ALU.max))
                    link(V.tensor_tensor(by_expert(hot), by_expert(hot), per_tile(g_m), ALU.is_equal))
                if part == 3:
                    link(V.scalar_tensor_tensor(g_a, g_b, -2.0, g_sc, ALU.mult, ALU.add))
                if part == 5:
                    link(V.tensor_tensor(g_b, g_b, g_c, ALU.add))
                if part == 6:
                    V.tensor_tensor(g_a, g_sc, g_b, ALU.mult)
                    V.tensor_copy(g_mask, g_b).then_inc(S["routed"], 1)

            def split_low(c):
                wait(dve, "nh_done", c + 1)
                V.tensor_tensor(nl[:, :], n2_t[:, bass.ts(c, CH)], nh[:, :].bitcast(fp32), ALU.subtract)\
                    .then_inc(S["nl_done"], 1)

            paired(dve, stage_a, 4, peeled=2)
            dve.wait_ge(S["wh_done"], 1)
            for stage, first, end in ((wstage, 0, W2), (w2stage, W2, NW)):
                V.tensor_tensor(wl[:, first:end, :], stage, wh[:, first:end, :].bitcast(fp32), ALU.subtract)\
                    .then_inc(S["wl_done"], 1)
            split_low(0)
            route(1, 0)

            def stage_b(c, e):
                n = E * c + e
                here = has(c)
                if here:
                    half = e // 4
                    wait(dve, f"wb_dma{half}", 16 * (c + 1))
                    wait(dve, "xh_done", n - 1)
                    wait(dve, "xl_done", n - 1)
                    V.tensor_tensor(tile4(xs[:, e % 2, :]), tile4(n2_t[:, bass.ts(c, CH)]),
                                    wb[:, half, :, e % 4 * P:(e % 4 + 1) * P], ALU.mult).then_inc(S["xs_done"], 1)
                if step_exists(c, e, 1):
                    k = (e - 1) % E
                    wait(dve, "xh_done", n)
                    wait(dve, "p3_done", n - 4)
                    V.tensor_tensor(xl[:, k % 4, :], xs[:, k % 2, :], xh[:, k % 4, :].bitcast(fp32), ALU.subtract)\
                        .then_inc(S["xl_done"], 1)
                if step_exists(c, e, 6):
                    k = (e - 6) % E
                    wait(dve, "p2_done", n - 5)
                    wait(dve, "m3_done", n - 5)
                    wait(dve, "acc_done", n - 9)
                    V.scalar_tensor_tensor(prod[:, k % 4, :], p2_bank[k % 2], bias[:, 8 + k:9 + k], m3[:, k % 4, :],
                                           ALU.add, ALU.mult).then_inc(S["prod_done"], 1)
                if at(c, NCH) and e == 6:
                    prepare_d()
                if here and e in (3, 6):
                    i = e // 3 - 1
                    wait(dve, "ga_done", 2 * c + i + 1)
                    wait(dve, "z_done", c)
                    if at(c, 0) and e == 3:
                        wait(dve, "b3_ready", 1)
                    V.tensor_tensor(gg[:, i, :], bank[7][:, :], ga, ALU.mult).then_inc(S["g_done"], 1)
                if e == 7 and chunk_follows(c):
                    wait(dve, "ab_done", 2 * (c + 1))
                    split_low(c + 1)
                if at(c, 0) and e < 6:
                    route(1, e + 1)
                if at(c, NCH) and e == 4:
                    recip3(0)
                if at(c, 0) and e == 7:
                    dve.wait_ge(S["small_dma"], 80)
                    V.tensor_tensor(bqk[:, :], bias[:, 16:17], bias[:, 17:18], ALU.add).then_inc(S["bqk_done"], 1)
                    dve.wait_ge(S["expclip"], 1)
                    link(V.tensor_scalar(sig[:, :], sig[:, :], 1.0, None, ALU.add))
                    link(V.reciprocal(sig[:, :], sig[:, :]))
                if e == 1 and has(c, 2):
                    wait(dve, "yt_done", c)
                    cols = bass.ts(c - 2, CH)
                    V.tensor_tensor(X[:, cols], X[:, cols], bank[7][:, :], ALU.add).then_inc(S["x2_done"], 1)
                if e == 2 and has(c, 2):
                    wait(dve, "x2_done", c)
                    stats_rows(2, c - 2)
                if e == 3 and has(c, 2):
                    stats_aggregate(2, c - 2)
                    stats_keep(2, c - 2)

            def recip3(part):
                tiles = slice(0, EARLY) if part == 0 else slice(EARLY, NT)
                dve.wait_ge(S["sqrt3"], part + 1)
                V.reciprocal(rs[2][:, tiles], sd[2][:, tiles]).then_inc(S["recip3"], 1)

            steps(dve, stage_b)

            def stage_c(c, p):
                if at(c, 1):
                    recip3(1)
                if has(c, 1):
                    wait(dve, "sc_pe", c)
                    wait(dve, "sub_done", c - 1)
                    raw = sc_bank[1 - p].rearrange("p (t k) -> p t k", t=TPC)
                    V.tensor_reduce(mx[:, :], raw, AX.X, ALU.max).then_inc(S["max_done"], 1)
                x3 = X[:, bass.ts(c - 3, CH)] if has(c, 3) else None
                if has(c, 3):
                    wait(dve, "o3_pe", c - 2)
                    V.tensor_tensor(x3, x3, bank[6][:, :], ALU.add).then_inc(S["x3_done"], 1)
                if has(c, 1):
                    wait(dve, "max_done", c)
                    wait(dve, "exp_done", 2 * (c - 2))
                    V.tensor_tensor(sc[:, 1 - p, :, :], raw, mx[:, :].rearrange("p (t a) -> p t a", a=1)
                                    .broadcast_to([P, TPC, SEQ]), ALU.subtract).then_inc(S["sub_done"], 1)
                if has(c, 3):
                    wait(dve, "x3_done", c - 2)
                    stats_rows(3, c - 3)
                    stats_aggregate(3, c - 3)
                if has(c, 5):
                    wait(dve, "centred4", c - 4)
                    V.tensor_reduce(row_max[:, bass.ts(c - 5, TPC)], tile4(centred[:, bass.ts(c - 5, CH)]), AX.X, ALU.max,
                                    apply_absolute_value=True).then_inc(S["row_max_done"], 1)
                if has(c, 1):
                    wait(dve, "exp_done", 2 * c)
                    wait(dve, "rinv_done", c - 1)
                    V.tensor_reduce(rsum[:, :], pr[1 - p], AX.X, ALU.add).then_inc(S["sum_done"], 1)
                if has(c, 3):
                    stats_keep(3, c - 3)
                if has(c, 1):
                    wait(dve, "sum_done", c)
                    wait(dve, "probs_done", c - 2)
                    V.reciprocal(rinv[:, 1 - p, :], rsum[:, :]).then_inc(S["rinv_done"], 1)

            paired(dve, stage_c, 5, head=6)

            dve.wait_ge(S["sqrt4"], 2)
            V.reciprocal(rs[3][:, :], sd[3][:, :]).then_inc(S["recip4"], 1)
            dve.wait_ge(S["recip4"], 1)
            dve.wait_ge(S["row_max_done"], NCH)
            steps_done = [0]

            def link_d(instruction):
                steps_done[0] += 1
                instruction.then_inc(S["qs_step"], 1)
                dve.wait_ge(S["qs_step"], steps_done[0])

            def quant_scale(j):
                dve.wait_ge(S["qs_all"], j + 1)
                link_d(V.scalar_tensor_tensor(qs[:, j, 2:3], qs[:, j, 1:2], 1.0 / QMAX, sig[:, j:j + 1], ALU.mult, ALU.mult))
                link_d(V.reciprocal(qs[:, j, 3:4], qs[:, j, 2:3]))

            link_d(V.tensor_tensor(norm_max, row_max, rs[3][:, :], ALU.mult))
            V.tensor_reduce(qs[:, 0, 0:1], norm_max, AX.X, ALU.max).then_inc(S["qs_own"], 1)
            quant_scale(0)
            V.tensor_scalar(step_scale[:, :], rs[3][:, :], qs[:, 0, 3:4], None, ALU.mult)
            V.tensor_scalar(wgu_i[:, 0:6], wgu_s[:, 0:6], qs[:, 0, 2:3], None, ALU.mult).then_inc(S["step_done"], 1)
            dve.wait_ge(S["step_done"], 1)

            def stage_d1(c, p):
                if has(c):
                    wait(dve, "norm_q_done", c + 1)
                    wait(dve, "qn_done", c)
                    V.tensor_scalar(norm_m, norm_q[:, p, :], MAGIC, MAGIC + QMAX, ALU.add, ALU.min)\
                        .then_inc(S["norm_m_done"], 1)
                if has(c):
                    wait(dve, "norm_m_done", c + 1)
                    wait(dve, "t4_done", c - 1)
                    V.tensor_scalar(qn[:, p, :], norm_m, MAGIC - QMAX - 1.0, MAGIC, ALU.max, ALU.subtract)\
                        .then_inc(S["qn_done"], 1)
                if has(c, 2):
                    for b in range(2):
                        wait(dve, "sg_done", 3 * (c - 2) + b + 2)
                        V.scalar_tensor_tensor(arena[:, bass.ds(((c - 2) * 3 + b) * CH, CH)], bank[4 + b][:, :],
                                               wgu_i[:, 3 + b:4 + b], sg[:, b * CH:(b + 1) * CH], ALU.mult, ALU.mult)\
                            .then_inc(S["h_done"], 1)
                if has(c, 3):
                    wait(dve, "h_done", 2 * (c - 2))
                    wait(dve, "h2_done", c - 2)
                    V.tensor_reduce(am[:, bass.ds(c - 3, 1)], arena[:, bass.ds((c - 3) * 3 * CH, 3 * CH)], AX.X, ALU.max,
                                    apply_absolute_value=True).then_inc(S["hmax_done"], 1)

            dve.wait_ge(S["wprep_done"], 1)
            paired(dve, stage_d1, 3, head=4)
            dve.wait_ge(S["hmax_done"], NCH)
            V.tensor_reduce(qs[:, 1, 0:1], am[:, :], AX.X, ALU.max).then_inc(S["qs_own"], 1)
            quant_scale(1)
            V.tensor_scalar(qs[:, 1, 4:5], qs[:, 1, 2:3], -QMAX - 1.0, None, ALU.mult)
            V.tensor_scalar(qs[:, 1, 5:6], qs[:, 1, 2:3], QMAX, None, ALU.mult)
            dve.wait_ge(S["wprep_done"], 1)
            V.tensor_scalar(down_scale[:, :], down_scale[:, :], qs[:, 1, 2:3], None, ALU.mult).then_inc(S["qs_dve"], 2)
            dve.wait_ge(S["qs_dve"], 2)

            def stage_d2(c, p):
                if has(c):
                    hid = arena[:, bass.ds(c * 3 * CH, 3 * CH)]
                    V.tensor_scalar(hid, hid, qs[:, 1, 4:5], qs[:, 1, 5:6], ALU.max, ALU.min).then_inc(S["hclamp_done"], 1)
                if has(c, 2):
                    wait(dve, "hmagic_done", c - 1)
                    wait(dve, "down_done", c - 3)
                    V.tensor_scalar(hq[:, p, 0:2 * CH], arena[:, bass.ds((c - 2) * 3 * CH, 2 * CH)], MAGIC, None,
                                    ALU.subtract).then_inc(S["hq_dve"], 1)
                if has(c, 3):
                    wait(dve, "down_done", c - 2)
                    wait(dve, "added_done", c - 4)
                    V.tensor_tensor(tile4(scaled[:, 1 - p, :]), tile4(down_bank[1 - p]),
                                    down_scale[:, :].rearrange("p (a n) -> p a n", a=1).broadcast_to([P, TPC, P]),
                                    ALU.mult).then_inc(S["scaled_done"], 1)

            paired(dve, stage_d2, 3, head=6)

        @block.gpsimd
        def _(pool):
            G = nc.gpsimd

            G.memset(eps_t[:, :], EPS)
            G.memset(magic_t[:, :], MAGIC)
            G.memset(minus_magic_t[:, :], -MAGIC).then_inc(S["act_consts"], 1)
            G.memset(mk[:, :], 0.0)
            G.memset(b3s[:, :, :], 0.0)
            pool.wait_ge(S["consts"], 48)
            G.tensor_copy(id16[:, :], id32[:, :]).then_inc(S["pool_consts"], 1)
            pool.wait_ge(S["pool_consts"], 1)

            count = [0]

            def link(instruction):
                count[0] += 1
                instruction.then_inc(S["b3_step"], 1)
                pool.wait_ge(S["b3_step"], count[0])

            def prepare_b3(part):
                if part == 0:
                    pool.wait_ge(S["small_dma"], 80)
                    rest = b3a
                else:
                    rest = b3b
                link(G.tensor_copy(b3h[:, :], rest))
                if part < 2:
                    link(G.tensor_tensor(b3b, rest, b3h[:, :], ALU.subtract))
                of_part = b3c if part == 0 else b3a
                link(G.tensor_scalar(of_part, b3h[:, :], pick[:, part:part + 1], None, ALU.mult))
                if part > 0:
                    link(G.tensor_tensor(b3c, b3c, b3a, ALU.add))
                if part == 2:
                    G.tensor_tensor(b3s[0:24, :, :], b3c.rearrange("p (a n) -> p a n", a=1).broadcast_to([24, E, P]),
                                    pick[:, 3:3 + E].rearrange("p (e a) -> p e a", a=1).broadcast_to([24, E, P]),
                                    ALU.mult).then_inc(S["b3_ready"], 1)

            def per_token(ap):
                return ap.rearrange("p (t a) -> p t a", a=1).broadcast_to([P, TPC, P])

            def normalise(dst, mean, inverse, c, centred, done):
                G.tensor_tensor(tile4(dst), tile4(X[:, bass.ts(c, CH)]), mean.broadcast_to([P, TPC, P]), ALU.subtract)\
                    .then_inc(S[centred], 1)
                pool.wait_ge(S[centred], c + 1)
                G.tensor_tensor(tile4(dst), tile4(dst), per_token(inverse), ALU.mult).then_inc(S[done], 1)

            def stage_a(c, p):
                if has(c):
                    wait(pool, "xn_done", c + 1)
                    cols = bass.ts(c, CH)
                    G.tensor_tensor(X[:, cols], X[:, cols], xn[:, p, :], ALU.add).then_inc(S["base_done"], 1)
                if has(c, 3):
                    wait(pool, "recip2", c - 2)
                    wait(pool, "t2_done", c - 4)
                    normalise(n2[:, 1 - p, :], mv_a[:, 1, 1 - p, :, 0:1], rs_a[:, 1, 1 - p, :], c - 3, "centred1", "n2_done")
                if isinstance(c, int) and c in (16, 17, 18):
                    prepare_b3(c - 16)

            paired(pool, stage_a, 3, peeled=2)

            def stage_b(c, e):
                if has(c):
                    wait(pool, "silu_done", E * c + e + 1)
                    wait(pool, "hh_done", E * c + e + 1)
                    wait(pool, "p2_done", E * c + e - 1)
                    G.tensor_tensor(hl[:, e % 2, :], hid_b[:, e % 2, :], hh[:, e % 4, :].bitcast(fp32),
                                    ALU.subtract).then_inc(S["hl_done"], 1)
                if at(c, NCH) and e == 1:
                    pool.wait_ge(S["xl_done"], E * NCH)
                    pool.wait_ge(S["nh_done"], NCH)
                    pool.wait_ge(S["xs_done"], E * NCH)
                    G.memset(ones, 1.0)
                    G.memset(pr_flat, 0.0).then_inc(S["pr_zero"], 1)
                    pool.wait_ge(S["recip3"], 1)
                    stage_c(0, 0)
                if step_exists(c, e, 4) and e != 4:
                    k, chunk = (e - 4) % E, c if e > 4 else c - 1
                    n = E * chunk + k
                    wait(pool, "prod_done", n + 1)
                    wait(pool, "acc_done", n - 1 if k == 1 else n)
                    if k == 5:
                        wait(pool, "zz_added", chunk + 1)
                    if k == 7:
                        wait(pool, "yt_done", chunk + 1)
                        if at(chunk, 0):
                            wait(pool, "weight_stored", 32)
                            wait(pool, "mask_stored", 32)
                    G.tensor_tensor(yf if k == 7 else yy, prod[:, 0, :] if k == 1 else yy, prod[:, k % 4, :], ALU.add)\
                        .then_inc(S["acc_done"], 2 if k == 1 else 1)
                    if k == 4:
                        wait(pool, "acc_done", n + 1)
                        wait(pool, "zz_done", chunk + 1)
                        G.tensor_tensor(yy, yy, zz, ALU.add).then_inc(S["zz_added"], 1)

            def stage_c(c, p):
                if has(c, 3):
                    wait(pool, "rinv_done", c - 2)
                    G.tensor_tensor(pr[1 - p], pr[1 - p], per_token(rinv[:, 1 - p, :]), ALU.mult).then_inc(S["probs_done"], 1)
                if at(c, 3):
                    pool.wait_ge(S["recip3"], 2)
                if has(c):
                    wait(pool, "t3_done", c - 1)
                    tiles = bass.ts(c, TPC)
                    normalise(n3[:, p, :], mv[2][:, tiles, 0:1], rs[2][:, tiles], c, "centred2", "n3_done")
                if has(c, 5):
                    wait(pool, "stats4", c - 4)
                    mean = mv[3][:, bass.ts(c - 5, TPC), 0:1].broadcast_to([P, TPC, P])
                    G.tensor_tensor(tile4(centred[:, bass.ts(c - 5, CH)]), tile4(X[:, bass.ts(c - 5, CH)]), mean, ALU.subtract)\
                        .then_inc(S["centred4"], 1)

            steps(pool, stage_b)
            paired(pool, stage_c, 5, head=6, first=1)

            pool.wait_ge(S["qs_own"], 1)
            G.partition_all_reduce(qs[:, 0, 1:2], qs[:, 0, 0:1], P, RMAX).then_inc(S["qs_all"], 1)
            pool.wait_ge(S["step_done"], 1)
            pool.wait_ge(S["wprep_done"], 1)

            def stage_d1(c, p):
                if has(c):
                    tiles = bass.ts(c, TPC)
                    wait(pool, "norm_m_done", c - 1)
                    G.tensor_tensor(tile4(norm_q[:, p, :]), tile4(centred[:, bass.ts(c, CH)]), per_token(step_scale[:, tiles]),
                                    ALU.mult).then_inc(S["norm_q_done"], 1)
                if has(c, 2):
                    wait(pool, "up_done", c - 1)
                    G.tensor_tensor(arena[:, bass.ds(((c - 2) * 3 + 2) * CH, CH)], up_2, sg[:, 2 * CH:3 * CH], ALU.mult)\
                        .then_inc(S["h2_done"], 1)

            paired(pool, stage_d1, 2, head=4)
            pool.wait_ge(S["qs_own"], 2)
            G.partition_all_reduce(qs[:, 1, 1:2], qs[:, 1, 0:1], P, RMAX).then_inc(S["qs_all"], 1)
            with pool.Fori(0, NCH // 2) as j:
                for p in range(2):
                    wait(pool, "scaled_done", 2 * j + p + 1)
                    cols = bass.ts(2 * j + p, CH)
                    G.tensor_tensor(X[:, cols], X[:, cols], scaled[:, p, :], ALU.add).then_inc(S["added_done"], 1)


def step_exists(c, e, lag):
    return not isinstance(c, int) or 0 <= E * c + e - lag < E * NCH


def chunk_follows(c):
    return not isinstance(c, int) or c < NCH - 1


def steps(engine, step):
    for n in range(E + E // 2):
        step(n // E, n % E)
    with engine.Fori(1, NCH - 1) as c:
        for e in range(E // 2, E):
            step(c, e)
        for e in range(E // 2):
            step(c + 1, e)
    for n in range(E * (NCH - 1) + E // 2, E * (NCH + 2)):
        step(n // E, n % E)


def kernel(x, ctx_1024, L0_ffn_gate_w, L0_ffn_w1, L0_ffn_b1, L0_ffn_w2, L0_ffn_b2, L0_ffn_w3, L0_ffn_b3, L0_ffn_sw1,
           L0_ffn_sw2, L0_ffn_sw3, L1_xattn_Wq, L1_xattn_bq, L1_xattn_qk_b, L1_xattn_Wv, L1_xattn_bv, L1_ffn_clip_x,
           L1_ffn_clip_down, L1_ffn_w_gate, L1_ffn_w_up, L1_ffn_w_down):
    import numpy as np
    import concourse.bacc as bacc
    from concourse.bass_utils import run_bass_kernel_spmd

    f32 = np.float32
    ctx2 = np.ascontiguousarray(np.asarray(ctx_1024).reshape(TOK, P).T)
    blocks = [L0_ffn_w1[e].T for e in range(E)] + [L0_ffn_w3[e].T for e in range(E)]
    blocks += [L0_ffn_sw1[i * P:(i + 1) * P].T for i in range(2)] + [L0_ffn_sw2[i * P:(i + 1) * P].T for i in range(2)]
    blocks += [L0_ffn_w2[e].T for e in range(E)]
    wall = np.stack([np.asarray(b) for b in blocks], axis=1)
    sw3T = np.stack([np.asarray(L0_ffn_sw3[:, i * P:(i + 1) * P].T) for i in range(2)], axis=1)
    biases = np.concatenate([np.asarray(a) for a in (L0_ffn_b1.T, L0_ffn_b2.T, L1_xattn_bq[:, None],
                                                     L1_xattn_qk_b[:, None], L1_xattn_bv[:, None])], axis=1)
    wgu = np.zeros((P, 2 * NB_FFN, P), f32)
    for j, w in enumerate((L1_ffn_w_gate, L1_ffn_w_up)):
        for b in range(NB_FFN):
            rows = np.asarray(w[b * P:min((b + 1) * P, I_FFN)])
            wgu[:rows.shape[0], j * NB_FFN + b, :] = rows
    wd = np.zeros((P, NB_FFN * P), f32)
    wd[:, :I_FFN] = np.asarray(L1_ffn_w_down)
    ident = np.eye(P, dtype=f32)
    s, t = np.arange(P)[:, None], np.arange(P)[None, :]
    causal = ((s // SEQ == t // SEQ) & (s <= t)).astype(f32)
    down8 = np.tile(np.arange(E, 0, -1, dtype=f32), (P, 1))
    pick = np.zeros((3 * E, 3 + E), f32)
    for r in range(3 * E):
        pick[r, r // E] = 1.0
        pick[r, 3 + r % E] = 1.0
    ins = dict(
        x=np.asarray(x).reshape(TOK, P), ctxT=ctx2, wall=wall, sw3T=sw3T, biases=biases,
        b3rep=np.concatenate([np.asarray(L0_ffn_b3)] * 3, axis=0), b3pick=pick, gateT=np.asarray(L0_ffn_gate_w).T,
        wqT=np.asarray(L1_xattn_Wq).T, wvT=np.asarray(L1_xattn_Wv).T, wgu=wgu.reshape(P, -1), wd=wd,
        clips=np.concatenate([np.asarray(L1_ffn_clip_x), np.asarray(L1_ffn_clip_down)]), ident=ident, causal=causal,
        down8=down8)
    ins = {k: np.ascontiguousarray(v) for k, v in ins.items()}
    nc = bacc.Bacc("TRN2", target_bir_lowering=False, num_devices=1, dynamic_dma_scratch_size=1024)
    args = {k: nc.dram_tensor(f"in_{k}", v.shape, mybir.dt.from_np(v.dtype), kind="ExternalInput").ap() for k, v in ins.items()}
    args["out"] = nc.dram_tensor("out", (TOK, P), fp32, kind="ExternalOutput").ap()
    build(nc, **args)
    r = run_bass_kernel_spmd(nc, [{f"in_{k}": v for k, v in ins.items()}], core_ids=[0])
    return np.asarray(r.results[0]["out"]).reshape(P, SEQ, P)
```
